# Optimizing a Trainium2 kernel written in Bass

```python
import numpy as np
import jax
import jax.numpy as jnp

def _softmax(x, axis=-1):
    return jax.nn.softmax(x, axis=axis)

def _gelu(x):
    return jax.nn.gelu(x, approximate=True)

def _silu(x):
    return jax.nn.silu(x)

def _sigmoid(x):
    return jax.nn.sigmoid(x)

def _layernorm(x, axis=-1, eps=1e-05):
    m = jnp.mean(x, axis=axis, keepdims=True)
    v = jnp.var(x, axis=axis, keepdims=True)
    return (x - m) / jnp.sqrt(v + eps)

def _scatter_add(tgt, idx, src, axis=0):
    return tgt.at[idx].add(src)

def _segment_sum(src, seg, n):
    return jax.ops.segment_sum(src, seg, n)
kernel_name = 'mk_gnn_resnorm_d4_gnn_r8_ded740'

def setup_inputs(seed: int=0):
    np.random.seed(seed)
    _w = jnp.asarray

    def _rec_inputs():
        import jax
        import jax.numpy as jnp
        _gk = jax.random.key(seed)
        x = -0.0003713 + 1 * jax.random.normal(jax.random.fold_in(_gk, 1), (6250, 128), jnp.float32)
        src = jax.random.randint(jax.random.fold_in(_gk, 2), (100000,), 0, 6250, jnp.int32)
        dst = jax.random.randint(jax.random.fold_in(_gk, 3), (100000,), 0, 6250, jnp.int32)
        _o = jnp.argsort(dst, stable=True)
        src = src[_o]
        dst = dst[_o]
        edge_attr_128 = -8.16379e-05 + 0.999858 * jax.random.normal(jax.random.fold_in(_gk, 11), (100000, 128), jnp.float32)
        edge_attr_64 = -5.16925e-05 + 1.00005 * jax.random.normal(jax.random.fold_in(_gk, 12), (100000, 64), jnp.float32)
        return (x, src, dst, edge_attr_128, edge_attr_64)
    x, src, dst, edge_attr_128, edge_attr_64 = _rec_inputs()

    def _L0_gnn_setup():
        import jax, jax.numpy as jnp
        import numpy as np
        NEG_SLOPE = 0.2
        key = jax.random.key(seed)
        ks = jax.random.split(key, 10)
        N, E, D, ED = (12500, 200000, 128, 64)
        x = jax.random.normal(ks[0], (N, D), dtype=jnp.float32)
        edge_index = jax.random.randint(ks[1], (2, E), 0, N, dtype=jnp.int32)
        edge_attr = jax.random.normal(ks[2], (E, ED), dtype=jnp.float32)
        s = 1.0 / np.sqrt(D)
        W = jax.random.normal(ks[3], (D, D), dtype=jnp.float32) * s
        att_src = jax.random.normal(ks[4], (D,), dtype=jnp.float32) * s
        att_dst = jax.random.normal(ks[5], (D,), dtype=jnp.float32) * s
        bias = jnp.zeros((D,), dtype=jnp.float32)
        We = jax.random.normal(ks[6], (ED, D), dtype=jnp.float32) / np.sqrt(ED)
        be = jnp.zeros((D,), dtype=jnp.float32)
        return {'x': x, 'edge_index': edge_index, 'edge_attr': edge_attr, 'W': W, 'att_src': att_src, 'att_dst': att_dst, 'bias': bias, 'We': We, 'be': be}
    _L0_gnn_all = _L0_gnn_setup()
    _L0_gnn_in = {k: v for k, v in _L0_gnn_all.items() if k in ('W', 'att_src', 'att_dst', 'bias', 'We', 'be')}
    del _L0_gnn_all

    def _L1_gnn_setup():
        import jax, jax.numpy as jnp
        import numpy as np
        LOG2 = 0.6931471824645996

        def ssp(x):
            return jax.nn.softplus(x) - LOG2
        N, M, F = (6250, 100000, 128)
        key = jax.random.key(seed)
        ks = jax.random.split(key, 12)

        def glorot(k, shape):
            lim = np.sqrt(6.0 / (shape[0] + shape[1])).astype(np.float32)
            return jax.random.uniform(k, shape, jnp.float32, -lim, lim)
        return {'node': jax.random.normal(ks[0], (N, F), jnp.float32), 'edge': jax.random.normal(ks[1], (M, F), jnp.float32), 'edge_index': jax.random.randint(ks[2], (2, M), 0, N, jnp.int32), 'Wn': glorot(ks[3], (F, 128)), 'We1': glorot(ks[4], (F, 128)), 'be1': jnp.zeros((128,), jnp.float32), 'We2': glorot(ks[5], (128, 128)), 'be2': jnp.zeros((128,), jnp.float32), 'W2': glorot(ks[6], (128, 128)), 'b2': jnp.zeros((128,), jnp.float32), 'W3': glorot(ks[7], (128, 128)), 'b3': jnp.zeros((128,), jnp.float32)}
    _L1_gnn_all = _L1_gnn_setup()
    _L1_gnn_in = {k: v for k, v in _L1_gnn_all.items() if k in ('Wn', 'We1', 'be1', 'We2', 'be2', 'W2', 'b2', 'W3', 'b3')}
    del _L1_gnn_all

    def _L2_gnn_setup():
        import jax, jax.numpy as jnp
        import numpy as np
        N_NODES = 12500
        key = jax.random.key(seed)
        k1, k2, k3 = jax.random.split(key, 3)
        x = jax.random.normal(k1, (N_NODES, 128), dtype=jnp.float32)
        edge_index = jax.random.randint(k2, (2, 200000), 0, N_NODES, dtype=jnp.int64)
        W = jax.random.normal(k3, (128, 128), dtype=jnp.float32) * 0.05
        b = jnp.zeros((128,), dtype=jnp.float32)
        return {'x': x, 'edge_index': edge_index, 'W': W, 'b': b}
    _L2_gnn_all = _L2_gnn_setup()
    _L2_gnn_in = {k: v for k, v in _L2_gnn_all.items() if k in ('W', 'b')}
    del _L2_gnn_all

    def _L3_gnn_setup():
        import jax, jax.numpy as jnp
        import numpy as np
        N_NODES = 1250
        N_EDGES = 80000
        D_IN = 128
        D_HID = 128
        key = jax.random.key(seed)
        k_x, k_e, k_w1, k_w2 = jax.random.split(key, 4)
        x = jax.random.normal(k_x, (N_NODES, D_IN), dtype=jnp.float32)
        edge_index = jax.random.randint(k_e, (2, N_EDGES), 0, N_NODES, dtype=jnp.int32)
        s1 = 1.0 / np.sqrt(D_IN)
        s2 = 1.0 / np.sqrt(D_HID)
        W1 = jax.random.normal(k_w1, (D_IN, D_HID), dtype=jnp.float32) * s1
        b1 = jnp.zeros((D_HID,), dtype=jnp.float32)
        W2 = jax.random.normal(k_w2, (D_HID, D_HID), dtype=jnp.float32) * s2
        b2 = jnp.zeros((D_HID,), dtype=jnp.float32)
        return {'x': x, 'edge_index': edge_index, 'W1': W1, 'b1': b1, 'W2': W2, 'b2': b2}
    _L3_gnn_all = _L3_gnn_setup()
    _L3_gnn_in = {k: v for k, v in _L3_gnn_all.items() if k in ('W1', 'b1', 'W2', 'b2')}
    del _L3_gnn_all
    return {'x': x, 'src': src, 'dst': dst, 'edge_attr_128': edge_attr_128, 'edge_attr_64': edge_attr_64, 'L0_gnn_W': _L0_gnn_in['W'], 'L0_gnn_att_src': _L0_gnn_in['att_src'], 'L0_gnn_att_dst': _L0_gnn_in['att_dst'], 'L0_gnn_bias': _L0_gnn_in['bias'], 'L0_gnn_We': _L0_gnn_in['We'], 'L0_gnn_be': _L0_gnn_in['be'], 'L1_gnn_Wn': _L1_gnn_in['Wn'], 'L1_gnn_We1': _L1_gnn_in['We1'], 'L1_gnn_be1': _L1_gnn_in['be1'], 'L1_gnn_We2': _L1_gnn_in['We2'], 'L1_gnn_be2': _L1_gnn_in['be2'], 'L1_gnn_W2': _L1_gnn_in['W2'], 'L1_gnn_b2': _L1_gnn_in['b2'], 'L1_gnn_W3': _L1_gnn_in['W3'], 'L1_gnn_b3': _L1_gnn_in['b3'], 'L2_gnn_W': _L2_gnn_in['W'], 'L2_gnn_b': _L2_gnn_in['b'], 'L3_gnn_W1': _L3_gnn_in['W1'], 'L3_gnn_b1': _L3_gnn_in['b1'], 'L3_gnn_W2': _L3_gnn_in['W2'], 'L3_gnn_b2': _L3_gnn_in['b2']}

def reference(x, src, dst, edge_attr_128, edge_attr_64, L0_gnn_W, L0_gnn_att_src, L0_gnn_att_dst, L0_gnn_bias, L0_gnn_We, L0_gnn_be, L1_gnn_Wn, L1_gnn_We1, L1_gnn_be1, L1_gnn_We2, L1_gnn_be2, L1_gnn_W2, L1_gnn_b2, L1_gnn_W3, L1_gnn_b3, L2_gnn_W, L2_gnn_b, L3_gnn_W1, L3_gnn_b1, L3_gnn_W2, L3_gnn_b2):
    import jax
    import jax.numpy as jnp

    def _L0_gnn_ref(x, edge_index, edge_attr, W, att_src, att_dst, bias, We, be):
        import jax, jax.numpy as jnp
        import numpy as np
        NEG_SLOPE = 0.2
        N = x.shape[0]
        edge_feat = edge_attr @ We + be
        h = x @ W
        loop = jnp.arange(N, dtype=edge_index.dtype)
        src = jnp.concatenate([edge_index[0], loop])
        dst = jnp.concatenate([edge_index[1], loop])
        a_s = h @ att_src
        a_d = h @ att_dst
        e = jax.nn.leaky_relu(a_s[src] + a_d[dst], NEG_SLOPE)
        seg_max = jax.ops.segment_max(e, dst, num_segments=N)
        e = jnp.exp(e - seg_max[dst])
        denom = jax.ops.segment_sum(e, dst, num_segments=N)
        alpha = e / (denom[dst] + 1e-16)
        out = jax.ops.segment_sum(h[src] * alpha[:, None], dst, num_segments=N)
        return out + bias

    def _L1_gnn_ref(node, edge, edge_index, Wn, We1, be1, We2, be2, W2, b2, W3, b3):
        import jax, jax.numpy as jnp
        import numpy as np
        LOG2 = 0.6931471824645996

        def ssp(x):
            return jax.nn.softplus(x) - LOG2
        N = node.shape[0]
        xn = node @ Wn
        f = ssp(edge @ We1 + be1)
        f = f @ We2 + be2
        msg = xn[edge_index[1]] * f
        agg = jax.ops.segment_sum(msg, edge_index[0], num_segments=N)
        h = ssp(agg @ W2 + b2)
        h = h @ W3 + b3
        return node + h

    def _L2_gnn_ref(x, edge_index, W, b):
        import jax, jax.numpy as jnp
        import numpy as np
        N_NODES = 12500
        N = x.shape[0]
        h = x @ W.T
        loops = jnp.arange(N, dtype=edge_index.dtype)
        src = jnp.concatenate([edge_index[0], loops])
        dst = jnp.concatenate([edge_index[1], loops])
        deg = jax.ops.segment_sum(jnp.ones_like(dst, dtype=h.dtype), dst, num_segments=N)
        dinv = jnp.where(deg > 0, jax.lax.rsqrt(deg), 0.0)
        norm = dinv[src] * dinv[dst]
        msgs = h[src] * norm[:, None]
        out = jax.ops.segment_sum(msgs, dst, num_segments=N)
        return out + b

    def _L3_gnn_ref(x, edge_index, W1, b1, W2, b2):
        import jax, jax.numpy as jnp
        import numpy as np
        N_NODES = 1250
        N_EDGES = 80000
        D_IN = 128
        D_HID = 128
        src = edge_index[0]
        dst = edge_index[1]
        msgs = x[src]
        agg = jax.ops.segment_sum(msgs, dst, num_segments=x.shape[0])
        h = agg + x
        h = jax.nn.relu(h @ W1 + b1)
        out = h @ W2 + b2
        return out
    edge_index = jnp.stack([src, dst])
    x = _layernorm(x + _L0_gnn_ref(x, edge_index, edge_attr_64, L0_gnn_W, L0_gnn_att_src, L0_gnn_att_dst, L0_gnn_bias, L0_gnn_We, L0_gnn_be), axis=-1)
    x = _layernorm(x + _L1_gnn_ref(x, edge_attr_128, edge_index, L1_gnn_Wn, L1_gnn_We1, L1_gnn_be1, L1_gnn_We2, L1_gnn_be2, L1_gnn_W2, L1_gnn_b2, L1_gnn_W3, L1_gnn_b3), axis=-1)
    x = _layernorm(x + _L2_gnn_ref(x, edge_index, L2_gnn_W, L2_gnn_b), axis=-1)
    x = _layernorm(x + _L3_gnn_ref(x, edge_index, L3_gnn_W1, L3_gnn_b1, L3_gnn_W2, L3_gnn_b2), axis=-1)
    return x

_drawn_inputs = setup_inputs


def setup_inputs(seed=0):
    import zlib

    import numpy as np

    out = dict(_drawn_inputs(seed))
    spreads = {'L0_gnn_bias': (0.0, 0.1),
     'L0_gnn_be': (0.0, 0.1),
     'L1_gnn_be1': (0.0, 0.1),
     'L1_gnn_be2': (0.0, 0.1),
     'L1_gnn_b2': (0.0, 0.1),
     'L1_gnn_b3': (0.0, 0.1),
     'L2_gnn_b': (0.0, 0.1),
     'L3_gnn_b1': (0.0, 0.417),
     'L3_gnn_b2': (0.0, 0.321)}
    factors = {}
    for name, (base, spread) in spreads.items():
        noise = np.random.default_rng([zlib.crc32(name.encode()), seed]).standard_normal(out[name].shape)
        drawn = base * np.exp(spread * noise) if base else spread * noise
        out[name] = jnp.asarray(drawn.astype(out[name].dtype))
    for name, factor in factors.items():
        out[name] = (out[name] * factor).astype(out[name].dtype)
    return out
```

```python
from contextlib import ExitStack

import concourse.bass as bass
from concourse import mybir

F32, BF16, I32, U32 = mybir.dt.float32, mybir.dt.bfloat16, mybir.dt.int32, mybir.dt.uint32
ALU = mybir.AluOpType
ACT = mybir.ActivationFunctionType
AX = mybir.AxisListType

P = 128
N, E, D = 6250, 100000, 128
NB = -(-N // P)
LAST = N - (NB - 1) * P
GRP = 4
STEPS = -(-(E // P + 1 + NB - 1) // GRP) * GRP
TICKS = STEPS // GRP
SG = -(-STEPS // P)
SW = SG * P
EP, EJ = 125, E // 125
LOGN = 17
PLACES = 1 << LOGN
SF = PLACES // P
LOGF = SF.bit_length() - 1
SRC_BITS, EID_BITS = 13, 17
KEY_BASE = 0x40000000
KEY_MASK = KEY_BASE - 1
PAD_KEY = 0x7F000000
SIGN = 0x80000000
BIG = float(2 ** 100)
LOG2 = 0.6931471824645996
SLOPE = 0.2
EPS = 1e-5
RING = 32
ARENA_WORDS = 25900
COPY_FIRST = 26
COPY_J = 20


class Line:

    def __init__(self, ctx, nc, name):
        self.ctx, self.nc, self.name, self.items, self.phase = ctx, nc, name, [], 0
        self.new_phase()

    def new_phase(self):
        self.sem = self.ctx.enter_context(self.nc.semaphore(f"{self.name}_{self.phase}"))
        self.count, self.phase = 0, self.phase + 1

    def do(self, fn, *after, quiet=False):
        self.items.append((after, fn, None if quiet else (self.sem, 1)))
        if quiet:
            return None
        self.count += 1
        return (self.sem, self.count)

    def dma(self, fn, mark, *after):
        self.items.append((after, fn, (mark[0], 16)))
        return mark

    def play(self, eng):
        seen = {}
        for after, fn, inc in self.items:
            for sem, value in after:
                if seen.get(sem.name, 0) < value:
                    eng.wait_ge(sem, value)
                    seen[sem.name] = value
            if fn is None:
                continue
            ins = fn(eng)
            if inc:
                ins.then_inc(*inc)


def build_program(nc, A, out):
    with ExitStack() as ctx:
        def sb(name, shape, dt=F32):
            return ctx.enter_context(nc.sbuf_tensor(name, shape, dt))

        arena = sb("arena", [P, ARENA_WORDS])
        taken = [0]

        def sb_ring(name, shape, dt=F32):
            parts, free = shape[0], 1
            for n in shape[1:]:
                free *= n
            words = -(-free * (2 if dt == BF16 else 4) // 4)
            at = taken[0]
            taken[0] = at + words
            assert taken[0] <= ARENA_WORDS, (name, taken[0])
            view = arena[0:parts, at:at + words].bitcast(dt)[:, 0:free]
            if len(shape) == 3:
                view = view.rearrange("p (a b) -> p a b", a=shape[1])
            return view

        def dram(name, shape, dt=F32):
            return nc.dram_tensor(name, shape, dt, kind="Internal").ap()

        def sem(name):
            return ctx.enter_context(nc.semaphore(name))

        bank = [ctx.enter_context(nc.psum_tensor(f"bank{i}", [P, 512], F32)) for i in range(8)]
        V, S, T, G, Y = (Line(ctx, nc, n) for n in ("vector", "scalar", "tensor", "gpsimd", "sync"))

        def barrier(*marks):
            ends = [(l.sem, l.count) for l in (V, S, T, G) if l.count] + list(marks)
            for l in (V, S, T, G, Y):
                l.items.append((tuple(ends), None, None))
            for l in (V, S, T, G):
                l.new_phase()

        sorted_keys = [dram(f"sorted_keys{k}", [PLACES], U32) for k in range(2)]
        step_block = [dram(f"step_block{k}", [SW]) for k in range(2)]
        gat_table = dram("gat_table", [NB * P, D + 2])
        node_table = [dram(f"node_table{k}", [NB * P, D]) for k in range(3)]
        edge_table = dram("edge_table", [E, D + 1])

        iota_free = sb("iota_free", [P, P])
        iota_part = sb("iota_part", [P, 1])
        ident = sb("ident", [P, P])
        ident_bf = sb("ident_bf", [P, P], BF16)
        big_ident = sb("big_ident", [P, P], BF16)
        neg_big_row = sb("neg_big_row", [1, P], BF16)
        ones_row = sb("ones_row", [1, GRP * P], BF16)
        ones = sb("ones", [P, P])
        const_done = []

        def c(line, fn, *after):
            t = line.do(fn, *after)
            const_done.append(t)
            return t

        c_iota = c(G, lambda e: e.iota(iota_free[:, :], [[1, P]], base=0, channel_multiplier=0,
                                       allow_small_or_imprecise_dtypes=True))
        c_part = c(G, lambda e: e.iota(iota_part[:, :], [[0, 1]], base=0, channel_multiplier=1,
                                       allow_small_or_imprecise_dtypes=True))
        c_ident = c(V, lambda e: e.tensor_scalar(ident[:, :], iota_free[:, :], iota_part[:, 0:1], None, ALU.is_equal),
                    c_iota, c_part)
        c(V, lambda e: e.tensor_copy(ident_bf[:, :], ident[:, :]), c_ident)
        c(V, lambda e: e.tensor_scalar(big_ident[:, :], ident[:, :], BIG, None, ALU.mult), c_ident)
        c(V, lambda e: e.memset(neg_big_row[:, :], -BIG))
        c(V, lambda e: e.memset(ones_row[:, :], 1.0))
        c(V, lambda e: e.memset(ones[:, :], 1.0))

        x_sb = sb("x_sb", [P, NB, D])
        index_sb = {k: sb_ring(f"index_{k}", [EP, EJ], U32) for k in ("src", "dst")}
        index_f = sb_ring("index_f", [EP, EJ])
        m_index = (sem("index_loaded"), 32)
        for k in ("src", "dst"):
            Y.dma(lambda e, k=k: e.dma_start(index_sb[k][:, :].bitcast(I32), A[k].rearrange("(p j) -> p j", p=EP)),
                  m_index)
        z_x = V.do(lambda e: e.memset(x_sb[:, NB - 1, :], 0.0))
        m_x = (sem("x_loaded"), 32)
        full = (NB - 1) * P
        Y.dma(lambda e: e.dma_start(x_sb[:, 0:NB - 1, :], A["x"][0:full, :].rearrange("(b p) d -> p b d", p=P)), m_x)
        Y.dma(lambda e: e.dma_start(x_sb[0:LAST, NB - 1, :], A["x"][full:N, :]), m_x, z_x)
        mats = {}
        rows = {}
        m_w = (sem("weights_loaded"), 0)
        n_w = 0
        for name in ("L0_gnn_W", "L1_gnn_Wn", "L1_gnn_We1", "L1_gnn_We2", "L1_gnn_W2", "L1_gnn_W3",
                     "L2_gnn_W", "L3_gnn_W1", "L3_gnn_W2"):
            mats[name] = sb("w_" + name, [P, D])
            Y.dma(lambda e, n=name: e.dma_start(mats[n][:, :], A[n]), m_w)
            n_w += 1
        for name in ("L0_gnn_att_src", "L0_gnn_att_dst", "L0_gnn_bias", "L1_gnn_be2", "L1_gnn_b3",
                     "L2_gnn_b", "L3_gnn_b2"):
            rows[name] = sb("r_" + name, [P, D])
            Y.dma(lambda e, n=name: e.dma_start(rows[n][:, :], A[n].rearrange("(o d) -> o d", o=1).to_broadcast([P, D])), m_w)
            n_w += 1
        cols = {}
        for name in ("L1_gnn_be1", "L1_gnn_b2", "L3_gnn_b1"):
            cols[name] = sb("c_" + name, [P, 1])
            Y.dma(lambda e, n=name: e.dma_start(cols[n][:, :], A[n].rearrange("(d o) -> d o", o=1)), m_w)
            n_w += 1
        m_w = (m_w[0], 16 * n_w)

        copy_tile = [sb_ring(f"copy_tile{i}", [EP, COPY_J, D + 1]) for i in range(2)]
        copy_in = [sem(f"copy_in{i}") for i in range(2)]
        copy_out = [sem(f"copy_out{i}") for i in range(2)]
        edges = A["edge_attr_128"].rearrange("(p j) d -> p j d", p=EP)
        edges_dst = edge_table.rearrange("(p j) d -> p j d", p=EP)
        n_copy = EJ // COPY_J

        def copy_edge_tile(n):
            i, turn, j = n % 2, n // 2, n * COPY_J
            tile = copy_tile[i]
            free = [(copy_out[i], 16 * turn)] if turn else []
            got = Y.dma(lambda e: e.dma_start(tile[:, :, 0:D], edges[:, j:j + COPY_J, :]),
                        (copy_in[i], 16 * (turn + 1)), *free)
            put = G.do(lambda e: e.tensor_copy(tile[:, :, D].bitcast(U32), index_sb["dst"][:, j:j + COPY_J]),
                       m_index, *free)
            return got, put

        def store_edge_tile(n, got, put):
            i, turn, j = n % 2, n // 2, n * COPY_J
            return Y.dma(lambda e: e.dma_start(edges_dst[:, j:j + COPY_J, :], copy_tile[i][:, :, :]),
                         (copy_out[i], 16 * (turn + 1)), got, put)

        def copy_edges(first, last):
            loads = [copy_edge_tile(first)]
            for n in range(first, last):
                if n + 1 < last:
                    loads.append(copy_edge_tile(n + 1))
                copied.append(store_edge_tile(n, *loads[-2 if n + 1 < last else -1]))

        copied = []

        gat_w = sb_ring("gat_w", [P, D + 2])
        att_prod = sb_ring("att_prod", [P, D])
        acc = sb("acc", [P, NB + 1, D + 2])
        dst_part = sb("dst_part", [P, NB + 1])
        xt = [sb(f"xt{k}", [P, GRP * P]) for k in range(2)]
        m_gat_table = (sem("gat_table_out"), 16)

        def build_gat_table():
            w0 = S.do(lambda e: e.copy(gat_w[:, 0:D], mats["L0_gnn_W"][:, :]), m_w)
            t = V.do(lambda e: e.tensor_tensor_reduce(out=att_prod[:, :], in0=mats["L0_gnn_W"][:, :],
                                                      in1=rows["L0_gnn_att_src"][:, :], scale=1.0, scalar=0.0,
                                                      op0=ALU.mult, op1=ALU.add, accum_out=gat_w[:, D:D + 1]), m_w)
            t = V.do(lambda e: e.tensor_tensor_reduce(out=att_prod[:, :], in0=mats["L0_gnn_W"][:, :],
                                                      in1=rows["L0_gnn_att_dst"][:, :], scale=1.0, scalar=0.0,
                                                      op0=ALU.mult, op1=ALU.add, accum_out=gat_w[:, D + 1:D + 2]), t)
            z = V.do(lambda e: e.memset(acc[:, NB, :], 0.0))
            z = V.do(lambda e: e.memset(acc[:, 0:NB, D:D + 1], 1.0), z)
            z = V.do(lambda e: e.memset(dst_part[:, NB:NB + 1], 0.0), z)
            sets = [list(range(b, min(b + 3, NB))) for b in range(0, NB, 3)]
            turned_x, evac, prod, kept = {}, {}, {}, {}
            for n in range(len(sets) + 1):
                if n < len(sets):
                    bs = sets[n]
                    for k, b in enumerate(bs):
                        turned_x[n] = T.do(lambda e, b=b, k=k: e.transpose(bank[5][:, k * P:(k + 1) * P], x_sb[:, b, :],
                                                                           ident[:, :]),
                                           m_x, c_ident, *([evac[n - 1]] if n else []), quiet=(k < len(bs) - 1))
                    wid = len(bs) * P
                    evac[n] = S.do(lambda e, n=n, wid=wid: e.copy(xt[n % 2][:, 0:wid], bank[5][:, 0:wid]),
                                   turned_x[n], *([prod[n - 2]] if n > 1 else []))
                if n:
                    n1 = n - 1
                    bs = sets[n1]
                    bk = bank[6 + n1 % 2]
                    for k, b in enumerate(bs):
                        prod[n1] = T.do(lambda e, k=k, n1=n1, bk=bk: e.matmul(
                            bk[:, k * (D + 2):(k + 1) * (D + 2)], xt[n1 % 2][:, k * P:(k + 1) * P], gat_w[:, :],
                            start=True, stop=True), evac[n1], w0, t, *([kept[n1 - 2]] if n1 > 1 else []),
                            quiet=(k < len(bs) - 1))
                    v = bk[:, 0:len(bs) * (D + 2)].rearrange("p (b d) -> p b d", d=D + 2)
                    b0, b1 = bs[0], bs[-1] + 1
                    S.do(lambda e, v=v, b0=b0, b1=b1: e.copy(acc[:, b0:b1, 0:D], v[:, :, 0:D]), prod[n1], z, quiet=True)
                    S.do(lambda e, v=v, b0=b0, b1=b1: e.copy(acc[:, b0:b1, D + 1], v[:, :, D]), quiet=True)
                    kept[n1] = S.do(lambda e, v=v, b0=b0, b1=b1: e.copy(dst_part[:, b0:b1], v[:, :, D + 1]))
            S.dma(lambda e: e.dma_start(gat_table.rearrange("(b p) d -> p b d", p=P), acc[:, 0:NB, :]),
                  m_gat_table, kept[len(sets) - 1], z)
            node_rows_done.append(kept[len(sets) - 1])
            node_rows_done.append(z)

        node_rows_done = []

        place = sb_ring("place", [P, SF], U32)
        place_x = sb_ring("place_x", [P, SF], U32)
        eid = sb_ring("eid", [EP, EJ], U32)
        c_place = c(G, lambda e: e.iota(place[:, :], [[1, SF]], base=0, channel_multiplier=SF))
        c_eid = c(G, lambda e: e.iota(eid[:, :], [[1, EJ]], base=0, channel_multiplier=EJ))
        sh = V.do(lambda e: e.tensor_scalar(place_x[:, :], place[:, :], 1, None, ALU.logical_shift_left), c_place)
        c_px = V.do(lambda e: e.tensor_tensor(place_x[:, :], place_x[:, :], place[:, :], ALU.bitwise_xor), sh)
        keys = [sb_ring(f"keys{i}", [P, SF], U32) for i in range(2)]
        turned = [sb_ring(f"turned{i}", [P, SF], U32) for i in range(2)]
        flip = sb_ring("flip", [P, SF], U32)
        copy_edges(0, COPY_FIRST)

        def substep(bufs, cur, m, after):
            a = bufs[cur][:, :].bitcast(F32).rearrange("p (n two m) -> p n two m", two=2, m=m)
            b = bufs[1 - cur][:, :].bitcast(F32).rearrange("p (n two m) -> p n two m", two=2, m=m)
            V.do(lambda e: e.tensor_tensor(b[:, :, 0, :], a[:, :, 0, :], a[:, :, 1, :], ALU.min), after, quiet=True)
            return V.do(lambda e: e.tensor_tensor(b[:, :, 1, :], a[:, :, 0, :], a[:, :, 1, :], ALU.max), after)

        def turn_over(src, dst, after):
            t = None
            for q in range(SF // P):
                bk = bank[q // 4]
                t = T.do(lambda e, q=q, bk=bk: e.transpose(
                    bk[:, (q % 4) * P:(q % 4 + 1) * P], src[:, q * P:(q + 1) * P].bitcast(F32), ident[:, :]),
                    after, c_ident, quiet=(q % 4 != 3))
                if q == 3:
                    half = t
            V.do(lambda e: e.tensor_copy(dst[:, 0:512].bitcast(F32), bank[0][:, :]), half, quiet=True)
            v = V.do(lambda e: e.tensor_copy(dst[:, 512:1024].bitcast(F32), bank[1][:, :]), t)
            return v

        def sort(hi, lo, lo_bits, out_list, mark, after):
            t = V.do(lambda e: e.memset(keys[0][:, :].bitcast(I32), PAD_KEY), *after)
            k0 = keys[0][0:EP, 0:EJ]
            t = V.do(lambda e: e.tensor_scalar(k0, hi[:, :], lo_bits, KEY_BASE, ALU.logical_shift_left, ALU.bitwise_or),
                     t, m_index)
            t = V.do(lambda e: e.tensor_tensor(k0, k0, lo[:, :], ALU.bitwise_or), t, c_eid)
            cur = 0
            for k in range(1, LOGN + 1):
                base = place if k == 1 else place_x
                f = V.do(lambda e, k=k, base=base: e.tensor_scalar(
                    flip[:, :], base[:, :], 31 - k if k < 31 else 0, SIGN, ALU.logical_shift_left, ALU.bitwise_and),
                    t, c_px)
                t = V.do(lambda e, cur=cur: e.tensor_tensor(keys[1 - cur][:, :], keys[cur][:, :], flip[:, :],
                                                            ALU.bitwise_xor), f)
                cur = 1 - cur
                if k > LOGF:
                    t = turn_over(keys[cur], turned[0], t)
                    tc = 0
                    for j in reversed(range(k - LOGF)):
                        t = substep(turned, tc, 1 << j, t)
                        tc = 1 - tc
                    t = turn_over(turned[tc], keys[cur], t)
                for j in reversed(range(min(k, LOGF))):
                    t = substep(keys, cur, 1 << j, t)
                    cur = 1 - cur
            return Y.dma(lambda e: e.dma_start(out_list.rearrange("(p f) -> p f", p=P), keys[cur][:, :]), mark, t), t

        off_bias = sb_ring("off_bias", [P, NB + 1])
        c_ob = c(G, lambda e: e.iota(off_bias[:, :], [[-P, NB + 1]], base=0, channel_multiplier=0,
                                     allow_small_or_imprecise_dtypes=True))
        c_ob = V.do(lambda e: e.tensor_scalar(off_bias[:, :], off_bias[:, :], 0.5, None, ALU.add), c_ob)
        step_no = sb_ring("step_no", [P, SG])
        c_sn = c(G, lambda e: e.iota(step_no[:, :], [[P, SG]], base=0, channel_multiplier=1,
                                     allow_small_or_imprecise_dtypes=True))
        sign_junk = sb_ring("sign_junk", [EP, EJ], BF16)
        below = sb_ring("below", [EP, NB + 1])
        offset = sb_ring("offset", [P, NB + 1])
        count = sb_ring("count", [P, NB])
        chunks_i = sb_ring("chunks_i", [P, NB], I32)
        chunks = sb_ring("chunks", [P, NB])
        zeros = sb("zeros", [P, NB + 1])
        c_z = c(V, lambda e: e.memset(zeros[:, :], 0.0))
        chunk_end = sb_ring("chunk_end", [P, NB])
        slack = sb_ring("slack", [P, NB])
        passed = sb_ring("passed", [P, SG, NB])
        passed_w = sb_ring("passed_w", [P, SG, NB])
        blk_col = [sb(f"blk_col{k}", [P, SG]) for k in range(2)]
        start_f = sb_ring("start_f", [P, SG])
        start_u = sb_ring("start_u", [P, SG], U32)
        window = sb_ring("window", [P, SW], U32)
        win_part = sb_ring("win_part", [P, SW], U32)
        win_f = sb_ring("win_f", [P, SW])
        blk_row = [sb(f"blk_row{k}", [P, SW]) for k in range(2)]
        blk_int = [sb(f"blk_int{k}", [1, SW], I32) for k in range(2)]
        local = [sb(f"local{k}", [P, SW]) for k in range(2)]
        pick = [sb(f"pick{k}", [P, SW], I32) for k in range(2)]

        def step_table(which, hi_index, hi_bits_low, list_ready, after):
            i = which
            blk = blk_col[i]
            f = V.do(lambda e: e.tensor_copy(index_f[:, :], hi_index[:, :]), m_index, *after)
            b0 = V.do(lambda e: e.memset(below[:, :], float(EJ)), *after)
            b1 = V.do(lambda e: e.memset(below[:, NB:NB + 1], -float(EJ)), b0)
            a = None
            for b in range(1, NB):
                a = S.do(lambda e, b=b: e.activation(sign_junk[:, :], index_f[:, :], ACT.Sign,
                                                     bias=off_bias[0:EP, b:b + 1], accum_out=below[:, b:b + 1]),
                         f, b1, c_ob, *([a] if a else []))
            mm = T.do(lambda e: e.matmul(bank[2][:, 0:NB + 1], ones[0:EP, :], below[:, :], start=True, stop=True),
                      a, b1, *const_done[5:8])
            t = V.do(lambda e: e.tensor_scalar(offset[:, :], bank[2][:, 0:NB + 1], -0.5, float(E) / 2,
                                               ALU.mult, ALU.add), mm)
            t = V.do(lambda e: e.tensor_tensor(count[:, :], offset[:, 1:NB + 1], offset[:, 0:NB], ALU.subtract), t)
            u = V.do(lambda e: e.tensor_scalar(chunks_i[:, :], count[:, :], float(P - 1), None, ALU.add), t)
            u = V.do(lambda e: e.tensor_scalar(chunks_i[:, :], chunks_i[:, :], 7, None, ALU.logical_shift_right), u)
            u = V.do(lambda e: e.tensor_copy(chunks[:, :], chunks_i[:, :]), u)
            w = V.do(lambda e: e.scalar_tensor_tensor(slack[:, :], chunks[:, :], -float(P), count[:, :],
                                                      ALU.mult, ALU.add), u)
            w = V.do(lambda e: e.tensor_tensor_scan(chunk_end[:, :], chunks[:, :], zeros[:, 0:NB], 0.0,
                                                    ALU.add, ALU.add), u, c_z)
            w = V.do(lambda e: e.tensor_tensor(passed[:, :, :], chunk_end[:, :].unsqueeze(1).to_broadcast([P, SG, NB]),
                                               step_no[:, :].unsqueeze(2).to_broadcast([P, SG, NB]), ALU.is_le),
                     w, c_sn)
            r = V.do(lambda e: e.tensor_reduce(blk[:, :], passed[:, :, :], AX.X, ALU.add), w)
            w = V.do(lambda e: e.tensor_tensor(passed_w[:, :, :], passed[:, :, :],
                                               slack[:, :].unsqueeze(1).to_broadcast([P, SG, NB]), ALU.mult), w)
            w = V.do(lambda e: e.tensor_reduce(start_f[:, :], passed_w[:, :, :], AX.X, ALU.add), w)
            w = V.do(lambda e: e.scalar_tensor_tensor(start_u[:, :], step_no[:, :], float(P), start_f[:, :],
                                                      ALU.mult, ALU.add), w)
            m1 = Y.dma(lambda e: e.dma_start(step_block[i].rearrange("(g p) -> p g", p=P), blk[:, :],
                                             allow_slow_non_contiguous=True), (sem(f"blk_out{i}"), 16), r)
            m2 = Y.dma(lambda e: e.dma_start(blk_row[i][:, :], step_block[i].rearrange("(o s) -> o s", o=1)
                                             .to_broadcast([P, SW])), (sem(f"blk_in{i}"), 16), m1)
            m3 = (sem(f"windows{i}"), 16 * SG)
            for g in range(SG):
                G.dma(lambda e, g=g: e.indirect_dma_start(
                    out=window[:, g * P:(g + 1) * P], out_offset=None,
                    in_=sorted_keys[i].rearrange("(n o) -> n o", o=1),
                    in_offset=bass.IndirectOffsetOnAxis(ap=start_u[:, g:g + 1], axis=0)), m3, w, list_ready)
            bi = V.do(lambda e: e.tensor_copy(blk_int[i][:, :], blk_row[i][0:1, :]), m2)
            last = []
            for part in range(2):
                if part == 0:
                    q = V.do(lambda e: e.tensor_scalar(win_part[:, :], window[:, :], KEY_MASK, hi_bits_low,
                                                       ALU.bitwise_and, ALU.logical_shift_right), m3)
                else:
                    q = V.do(lambda e: e.tensor_scalar(win_part[:, :], window[:, :], (1 << hi_bits_low) - 1, None,
                                                       ALU.bitwise_and), m3, *last)
                q = V.do(lambda e: e.tensor_copy(win_f[:, :], win_part[:, :]), q, *last)
                for g in range(SG):
                    bk = bank[3 + g // 4]
                    q2 = T.do(lambda e, g=g, bk=bk: e.transpose(bk[:, (g % 4) * P:(g % 4 + 1) * P],
                                                                win_f[:, g * P:(g + 1) * P], ident[:, :]), q, *last)
                res = []
                for h in range(2):
                    lo, hi = h * 512, min((h + 1) * 512, SW)
                    if part == 0:
                        res.append(V.do(lambda e, lo=lo, hi=hi, h=h: e.scalar_tensor_tensor(
                            local[i][:, lo:hi], blk_row[i][:, lo:hi], -float(P), bank[3 + h][:, 0:hi - lo],
                            ALU.mult, ALU.add), q2, m2))
                    else:
                        res.append(V.do(lambda e, lo=lo, hi=hi, h=h: e.tensor_copy(
                            pick[i][:, lo:hi], bank[3 + h][:, 0:hi - lo]), q2))
                last = res
            return last + [bi]

        build_gat_table()
        l1, after1 = sort(index_sb["dst"], index_sb["src"], SRC_BITS, sorted_keys[0], (sem("list0"), 16), [])
        t1 = step_table(0, index_sb["dst"], SRC_BITS, l1, [])
        copy_edges(COPY_FIRST, n_copy)
        l2, after2 = sort(index_sb["src"], eid, EID_BITS, sorted_keys[1], (sem("list1"), 16), [l1])
        t2 = step_table(1, index_sb["src"], EID_BITS, l2, t1)
        barrier(*copied[-2:], l2, m_index)
        taken[0] = 0

        slot_sem = [sem(f"slot{k}") for k in range(RING)]
        slot_uses = [0] * RING
        gathered = sb_ring("gathered", [P, RING, D + 2])
        idle_regs = {}

        def gather(slot, dst, table, index, *after):
            slot_uses[slot] += 1
            return G.dma(lambda e: e.indirect_dma_start(
                out=dst, out_offset=None, in_=table, in_offset=bass.IndirectOffsetOnAxis(ap=index, axis=0)),
                (slot_sem[slot], 16 * slot_uses[slot]), *after)

        def block_registers(which, tick):
            if tick % 4:
                return

            def load(e):
                if "regs" not in idle_regs:
                    idle_regs["regs"] = [e.register(f"block_reg{k}") for k in range(16)]
                    idle_regs["regs"] = [r.__enter__() if hasattr(r, "__enter__") else r for r in idle_regs["regs"]]
                i = tick * GRP
                return e.load(idle_regs["regs"], blk_int[which][0:1, i:i + 16])
            V.do(load, quiet=True)

        def block_sum(e, i, width):
            b = e.snap(idle_regs["regs"][i % 16], min_val=0, max_val=NB)
            return acc[:, bass.ds(b, 1), 0:width].rearrange("p o d -> p (o d)")

        def pipeline(n, stages):
            for t in range(n + len(stages) - 1):
                for k in reversed(range(len(stages))):
                    if 0 <= t - k < n:
                        stages[k](t - k)

        SWP = SW + 1
        pair = sb_ring("pair", [P, 2, SWP])
        self_max = sb_ring("self_max", [P, SW])
        same = sb_ring("same", [P, SW])
        degree_part = sb_ring("degree_part", [P, SW])
        block_hot = sb_ring("block_hot", [NB + 1, SW])
        self_logit = sb("self_logit", [P, NB + 1])
        self_tmp = sb("self_tmp", [P, NB + 1])
        part_t = sb_ring("part_t", [NB + 1, 2, P])

        t = V.do(lambda e: e.tensor_copy(self_tmp[:, NB:NB + 1], zeros[:, 0:1]))
        t = V.do(lambda e: e.tensor_tensor(self_tmp[:, 0:NB], acc[:, 0:NB, D + 1], dst_part[:, 0:NB], ALU.add), t)
        t = V.do(lambda e: e.scalar_tensor_tensor(self_logit[:, :], self_tmp[:, :], SLOPE, self_tmp[:, :],
                                                  ALU.mult, ALU.max), t)
        h = V.do(lambda e: e.tensor_scalar(block_hot[:, :], blk_row[0][0:NB + 1, :], iota_part[0:NB + 1, 0:1], None,
                                           ALU.is_equal), t)
        T.do(lambda e: e.transpose(bank[0][0:NB + 1, 0:P], dst_part[:, :], ident[:, :]), quiet=True)
        u = T.do(lambda e: e.transpose(bank[0][0:NB + 1, P:2 * P], self_logit[:, :], ident[:, :]), t)
        v = V.do(lambda e: e.tensor_copy(part_t[:, :, :], bank[0][0:NB + 1, 0:2 * P]
                                         .rearrange("p (a n) -> p a n", a=2)), u)
        half = SW // 2
        for a in range(2):
            for q in range(2):
                u = T.do(lambda e, a=a, q=q: e.matmul(bank[1 + 2 * a + q][:, 0:half], part_t[:, a, :],
                                                      block_hot[:, q * half:(q + 1) * half], start=True, stop=True), v, h)
        V.do(lambda e: e.memset(pair[:, :, 0:1], 0.0), quiet=True)
        for q in range(2):
            V.do(lambda e, q=q: e.tensor_copy(pair[:, 0, 1 + q * half:1 + (q + 1) * half], bank[1 + q][:, 0:half]),
                 u, quiet=True)
            V.do(lambda e, q=q: e.tensor_copy(self_max[:, q * half:(q + 1) * half], bank[3 + q][:, 0:half]), quiet=True)
        V.do(lambda e: e.memset(degree_part[:, :], 0.0), quiet=True)
        w = V.do(lambda e: e.memset(same[:, 0:1], 0.0))
        w = V.do(lambda e: e.tensor_tensor(same[:, 1:SW], blk_row[0][:, 1:SW], blk_row[0][:, 0:SW - 1], ALU.is_equal), w)
        v_prep = V.do(lambda e: e.tensor_scalar(same[:, :], same[:, :], 1.0, 1e30, ALU.subtract, ALU.mult), w)
        barrier()

        hot_bf = [sb_ring(f"hot_bf{k}", [P, GRP, P], BF16) for k in range(2)]
        hot_t = [sb_ring(f"hot_t{k}", [P, GRP, P]) for k in range(2)]
        hot = [sb_ring(f"hot{k}", [P, GRP, P]) for k in range(2)]
        small = {n: sb("s_" + n, [P, 4, GRP]) for n in ("top", "logit", "new", "old", "drop", "edge", "edge2", "weight", "scale")}

        oh, tr, msk, evc, mx, drp, pc, ez, wt, scl, hw, po, sm = ({} for _ in range(13))

        def slots(t):
            return [(t * GRP + s) % RING for s in range(GRP)]

        def landed(t):
            return [landed_at[t * GRP + s] for s in range(GRP)]

        landed_at = {}

        def get(d, t):
            return [d[t]] if t in d else []

        def gat_gather(t):
            for s, slot in enumerate(slots(t)):
                i = t * GRP + s
                landed_at[i] = gather(slot, gathered[:, slot, :], gat_table, pick[0][:, i:i + 1],
                                      m_gat_table, *get(po, t - RING // GRP))

        def gat_mask(t):
            i = t * GRP
            oh[t] = V.do(lambda e: e.tensor_tensor(
                hot_bf[t % 2][:, :, :], iota_free[:, :].unsqueeze(1).to_broadcast([P, GRP, P]),
                local[0][:, i:i + GRP].unsqueeze(2).to_broadcast([P, GRP, P]), ALU.is_equal), *get(msk, t - 2))
            for s in range(GRP):
                tr[t] = T.do(lambda e, s=s: e.transpose(bank[0][:, :].bitcast(BF16)[:, s * P:(s + 1) * P],
                                                        hot_bf[t % 2][:, s, :], ident_bf[:, :]),
                             oh[t], *get(evc, t - 1), quiet=(s < GRP - 1))
            bk = bank[2 + t % 2]
            T.do(lambda e: e.matmul(bk[:, :], neg_big_row[:, :], ones_row[:, :], start=True, stop=False),
                 *get(mx, t - 2), quiet=True)
            for s, slot in enumerate(slots(t)):
                o = bk[:, s * P:(s + 1) * P]
                T.do(lambda e, s=s, o=o: e.matmul(o, hot_bf[t % 2][:, s, :], big_ident[:, :], start=False, stop=False),
                     quiet=True)
                msk[t] = T.do(lambda e, s=s, o=o, slot=slot: e.matmul(
                    o, gathered[:, slot, D + 1:D + 2].to_broadcast([P, P]), ident[:, :], start=False, stop=(s == GRP - 1)),
                    landed_at[t * GRP + s], quiet=(s < GRP - 1))

        def gat_max(t):
            i, r = t * GRP, t % 4
            for s in range(GRP):
                evc[t] = S.do(lambda e, s=s: e.activation(hot_t[t % 2][:, s, :], bank[0][:, :].bitcast(BF16)
                                                          [:, s * P:(s + 1) * P], ACT.Copy,
                                                          accum_out=degree_part[:, i + s:i + s + 1]),
                              tr[t], *get(pc, t - 2), quiet=(s < GRP - 1))
            top, logit, new, old, drop = (small[n][:, r, :] for n in ("top", "logit", "new", "old", "drop"))
            adst, run = pair[:, 0, 1 + i:1 + i + GRP], pair[:, 1, 1 + i:1 + i + GRP]
            mx[t] = V.do(lambda e: e.tensor_reduce(top, bank[2 + t % 2][:, :].rearrange("p (s n) -> p s n", s=GRP),
                                                   AX.X, ALU.max), msk[t])
            q = V.do(lambda e: e.tensor_tensor(logit, top, adst, ALU.add), mx[t])
            q = V.do(lambda e: e.scalar_tensor_tensor(new, logit, SLOPE, logit, ALU.mult, ALU.max), q)
            q = V.do(lambda e: e.tensor_tensor(new, new, self_max[:, i:i + GRP], ALU.max), q)
            q = V.do(lambda e: e.tensor_tensor_scan(run, same[:, i:i + GRP], new, pair[:, 1, i:i + 1],
                                                    ALU.add, ALU.max), q)
            q = V.do(lambda e: e.tensor_tensor(old, pair[:, 1, i:i + GRP], same[:, i:i + GRP], ALU.add), q)
            q = V.do(lambda e: e.tensor_tensor(old, old, self_max[:, i:i + GRP], ALU.max), q)
            drp[t] = V.do(lambda e: e.tensor_tensor(drop, old, run, ALU.subtract), q, *get(scl, t - 4))

        def gat_pair(t):
            for s in range(GRP):
                i = t * GRP + s
                o = 2 * s
                pc[t] = T.do(lambda e, s=s, i=i, o=o: e.matmul(bank[1][:, o:o + 2], hot_t[t % 2][:, s, :],
                                                               pair[:, :, 1 + i], start=True, stop=True),
                             evc[t], drp[t], *get(ez, t - 1), quiet=(s < GRP - 1))

        def gat_weight(t):
            r, s0 = t % 4, slots(t)[0]
            edge, edge2, weight = (small[n][:, r, :] for n in ("edge", "edge2", "weight"))
            both = bank[1][:, 0:2 * GRP].rearrange("p (s a) -> p s a", a=2)
            q = V.do(lambda e: e.tensor_tensor(edge, both[:, :, 0], gathered[:, s0:s0 + GRP, D + 1], ALU.add),
                     pc[t], *landed(t))
            q = V.do(lambda e: e.scalar_tensor_tensor(edge2, edge, SLOPE, edge, ALU.mult, ALU.max), q, *get(wt, t - 4))
            ez[t] = V.do(lambda e: e.tensor_tensor(edge2, edge2, both[:, :, 1], ALU.subtract), q)
            q = V.do(lambda e: e.tensor_scalar(edge2, edge2, 0.0, None, ALU.min), ez[t])
            wt[t] = S.do(lambda e: e.activation(weight, edge2, ACT.Exp), q, *get(hw, t - 4))
            scl[t] = S.do(lambda e: e.activation(small["scale"][:, r, :], small["drop"][:, r, :], ACT.Exp),
                          drp[t], *get(sm, t - 4))

        def sum_place(t, s):
            return bank[4 + 2 * (t % 2) + s // 3][:, (s % 3) * (D + 2):(s % 3) * (D + 2) + D + 1]

        def gat_product(t):
            for s in range(GRP):
                i = t * GRP + s
                hw[t] = V.do(lambda e, s=s, i=i: e.tensor_scalar(
                    hot[t % 2][:, s, :], iota_free[:, :], local[0][:, i:i + 1], small["weight"][:, t % 4, s:s + 1],
                    ALU.is_equal, ALU.mult), wt[t], *get(po, t - 2), quiet=(s < GRP - 1))
            for s, slot in enumerate(slots(t)):
                o = sum_place(t, s)
                po[t] = T.do(lambda e, s=s, slot=slot, o=o: e.matmul(o, hot[t % 2][:, s, :], gathered[:, slot, 0:D + 1],
                                                                     start=True, stop=True),
                             hw[t], *landed(t), *get(sm, t - 2), quiet=(s < GRP - 1))

        def gat_sum(t):
            block_registers(0, t)
            q = None
            for s in range(GRP):
                i = t * GRP + s
                o = sum_place(t, s)

                def add(e, i=i, o=o, s=s):
                    a = block_sum(e, i, D + 1)
                    return e.scalar_tensor_tensor(a, a, small["scale"][:, t % 4, s:s + 1], o, ALU.mult, ALU.add)
                q = V.do(add, po[t], scl[t], *([q] if q else get(sm, t - 1)))
            sm[t] = q

        pipeline(TICKS, [gat_gather, gat_mask, gat_max, gat_pair, gat_weight, gat_product, gat_sum])
        barrier()

        sets = [list(range(b, min(b + GRP, NB))) for b in range(0, NB, GRP)]
        NS = len(sets)
        res = [sb_ring(f"res{k}", [P, GRP, D]) for k in range(4)]
        stats = sb("stats", [P, NB, 6])
        moments = sb("moments", [P, NB, 2])
        log_var = sb("log_var", [P, NB])
        rstd = sb("rstd", [P, NB])
        eps_col = sb("eps_col", [P, 1])
        w_eps = V.do(lambda e: e.memset(eps_col[:, :], EPS))

        def span(n):
            return sets[n][0], sets[n][-1] + 1

        class Norm:

            def __init__(self):
                self.mean, self.rs, self.x = {}, {}, {}

            def stats(self, n, after):
                q = after
                for k, b in enumerate(sets[n]):
                    p = V.do(lambda e, k=k, b=b: e.bn_stats(stats[:, b, :], res[n % 4][:, k, :]), q)
                    self.mean[n] = V.do(lambda e, b=b: e.bn_aggr(moments[:, b, :], stats[:, b, :]), p)

            def root(self, n):
                b0, b1 = span(n)
                q = S.do(lambda e: e.activation(log_var[:, b0:b1], moments[:, b0:b1, 1], ACT.Ln, bias=eps_col[:, 0:1]),
                         self.mean[n], w_eps)
                self.rs[n] = S.do(lambda e: e.activation(rstd[:, b0:b1], log_var[:, b0:b1], ACT.Exp, scale=-0.5), q)

            def scale(self, n):
                for k, b in enumerate(sets[n]):
                    self.x[n] = V.do(lambda e, k=k, b=b: e.tensor_scalar(
                        x_sb[:, b, :], res[n % 4][:, k, :], moments[:, b, 0:1], rstd[:, b:b + 1],
                        ALU.subtract, ALU.mult), self.rs[n], quiet=(k < len(sets[n]) - 1))

        class Dense:

            def __init__(self, bank_t, bank_o, buf):
                self.bt, self.bo, self.buf, self.tr, self.ev, self.mm, self.used = bank_t, bank_o, buf, {}, {}, {}, {}

            def turn(self, n, src, *after):
                for k, b in enumerate(sets[n]):
                    self.tr[n] = T.do(lambda e, k=k, b=b: e.transpose(self.bt[n % 2][:, k * P:(k + 1) * P], src(b),
                                                                      ident[:, :]),
                                      *after, *get(self.ev, n - 2), quiet=(k < len(sets[n]) - 1))

            def keep(self, n):
                wid = len(sets[n]) * P
                self.ev[n] = S.do(lambda e: e.copy(self.buf[n % 2][:, 0:wid], self.bt[n % 2][:, 0:wid]),
                                  self.tr[n], *get(self.mm, n - 2))

            def times(self, n, mat, bias_row=None):
                bk = self.bo[n % 2]
                cnt = len(sets[n])
                if bias_row is not None:
                    T.do(lambda e: e.matmul(bk[:, 0:cnt * P], ones[0:1, :],
                                            bias_row[0:1, :].unsqueeze(1).to_broadcast([1, cnt, D]),
                                            start=True, stop=False), *get(self.used, n - 2), quiet=True)
                for k in range(cnt):
                    self.mm[n] = T.do(lambda e, k=k: e.matmul(
                        bk[:, k * P:(k + 1) * P], self.buf[n % 2][:, k * P:(k + 1) * P], mat[:, :],
                        start=bias_row is None, stop=(bias_row is None or k == cnt - 1)),
                        self.ev[n], *get(self.used, n - 2), quiet=(k < cnt - 1))

            def columns(self, n, mat):
                wid = len(sets[n]) * P
                self.mm[n] = T.do(lambda e: e.matmul(self.bo[n % 2][:, 0:wid], mat[:, :], self.buf[n % 2][:, 0:wid],
                                                     start=True, stop=True), self.ev[n], *get(self.used, n - 2))

        inv_den = sb("inv_den", [P, NB])
        q = V.do(lambda e: e.tensor_scalar(inv_den[:, :], acc[:, 0:NB, D], 1e-16, None, ALU.add))
        v_den = V.do(lambda e: e.reciprocal(inv_den[:, :], inv_den[:, :]), q)
        deg_t = sb_ring("deg_t", [P, SG, P])
        group_hot = sb_ring("group_hot", [P, SG, NB])
        inv_sqrt_deg = sb("inv_sqrt_deg", [P, NB])
        for g in range(SG):
            u = T.do(lambda e, g=g: e.transpose(bank[g // 4][:, (g % 4) * P:(g % 4 + 1) * P],
                                                degree_part[:, g * P:(g + 1) * P], ident[:, :]))
        V.do(lambda e: e.tensor_copy(deg_t[:, 0:4, :], bank[0][:, :].rearrange("p (g n) -> p g n", n=P)), u, quiet=True)
        V.do(lambda e: e.tensor_copy(deg_t[:, 4:SG, :], bank[1][:, 0:(SG - 4) * P].rearrange("p (g n) -> p g n", n=P)),
             quiet=True)
        q = V.do(lambda e: e.tensor_tensor(group_hot[:, :, :], blk_col[0][:, :].unsqueeze(2).to_broadcast([P, SG, NB]),
                                           iota_free[:, 0:NB].unsqueeze(1).to_broadcast([P, SG, NB]), ALU.is_equal))
        for g in range(SG):
            u = T.do(lambda e, g=g: e.matmul(bank[2][:, 0:NB], deg_t[:, g, :], group_hot[:, g, :], start=(g == 0),
                                             stop=(g == SG - 1)), q)
        q = S.do(lambda e: e.activation(inv_sqrt_deg[:, :], bank[2][:, 0:NB], ACT.Ln, bias=1.0), u)
        s_deg = S.do(lambda e: e.activation(inv_sqrt_deg[:, :], inv_sqrt_deg[:, :], ACT.Exp, scale=-0.5), q)

        bias_fold, v_folds = {}, []
        for k, (mat, row) in enumerate((("L1_gnn_We2", "L1_gnn_be2"), ("L1_gnn_W3", "L1_gnn_b3"))):
            bias_fold[row] = sb("fold_" + row, [P, D])
            u = T.do(lambda e, k=k, mat=mat: e.matmul(bank[3][:, k * P:(k + 1) * P], ones[:, :], mats[mat][:, :],
                                                      start=True, stop=True), *v_folds[-1:])
            v_folds.append(None)
            v_fold = V.do(lambda e, k=k, row=row: e.scalar_tensor_tensor(
                bias_fold[row][:, :], bank[3][:, k * P:(k + 1) * P], -LOG2, rows[row][:, :], ALU.mult, ALU.add), u)
            v_folds[-1] = v_fold
        gcn_w = sb("gcn_w", [P, D])
        u = T.do(lambda e: e.transpose(bank[3][:, 2 * P:3 * P], mats["L2_gnn_W"][:, :], ident[:, :]), v_folds[-1])
        s_gcn = S.do(lambda e: e.copy(gcn_w[:, :], bank[3][:, 2 * P:3 * P]), u)

        xb = [sb_ring(f"xb{k}", [P, GRP, D]) for k in range(2)]
        rows_out = [sb_ring(f"rows_out{k}", [P, GRP, D]) for k in range(2)]
        norm, dense = Norm(), Dense(bank[4:6], bank[6:8], xt)
        table_sem = [sem(f"table{k}") for k in range(3)]
        rows_sem = [sem(f"rows{k}") for k in range(2)]
        zeroed, row_ready = {}, {}

        def n1_res(n):
            b0, b1 = span(n)
            q = V.do(lambda e: e.tensor_tensor(xb[n % 2][:, 0:b1 - b0, :], x_sb[:, b0:b1, :],
                                               rows["L0_gnn_bias"][:, :].unsqueeze(1).to_broadcast([P, b1 - b0, D]),
                                               ALU.add))
            for k, b in enumerate(sets[n]):
                p = V.do(lambda e, k=k, b=b: e.scalar_tensor_tensor(
                    res[n % 4][:, k, :], acc[:, b, 0:D], inv_den[:, b:b + 1], xb[n % 2][:, k, :], ALU.mult, ALU.add),
                    q, v_den)
            zeroed[n] = G.do(lambda e: e.memset(acc[:, b0:b1, 0:D], 0.0), p)
            norm.stats(n, p)

        def n1_rows(n):
            b0, b1 = span(n)
            wid = (b1 - b0) * P
            row_ready[n] = S.do(lambda e: e.copy(rows_out[n % 2][:, 0:b1 - b0, :],
                                                 dense.bo[n % 2][:, 0:wid].rearrange("p (b d) -> p b d", d=D)),
                                dense.mm[n], *([(rows_sem[n % 2], 16 * (n // 2))] if n > 1 else []))
            dense.used[n] = row_ready[n]
            Y.dma(lambda e: e.dma_start(node_table[0][b0 * P:b1 * P, :].rearrange("(b p) d -> p b d", p=P),
                                        rows_out[n % 2][:, 0:b1 - b0, :]),
                  (rows_sem[n % 2], 16 * (n // 2 + 1)), row_ready[n])

        pipeline(NS, [n1_res, norm.root, norm.scale,
                      lambda n: dense.turn(n, lambda b: x_sb[:, b, :], norm.x[n]), dense.keep,
                      lambda n: dense.times(n, mats["L1_gnn_Wn"]), n1_rows])
        table_marks = [(rows_sem[(NS - 1 - k) % 2], 16 * ((NS - 1 - k) // 2 + 1)) for k in range(2)]
        barrier()

        edge_row = sb_ring("edge_row", [P, RING // 2, D + 1])
        edge_sem = [sem(f"edge_slot{k}") for k in range(RING // 2)]
        edge_t = [sb_ring(f"edge_t{k}", [P, GRP * P]) for k in range(2)]
        magn = [sb_ring(f"magn{k}", [P, GRP * P]) for k in range(2)]
        plus = [sb_ring(f"plus{k}", [P, GRP * P]) for k in range(2)]
        message = [sb_ring(f"message{k}", [P, GRP, D]) for k in range(2)]
        hot1 = [sb_ring(f"hot1_{k}", [P, GRP, P]) for k in range(2)]
        be1 = cols["L1_gnn_be1"]
        edge_at = {}
        oh, tr, ev, hid, rel, sp, fil, msg, po, sm, xg = ({} for _ in range(11))
        ER = RING // 2

        def cf_edges(t):
            for s in range(GRP):
                i = t * GRP + s
                slot = i % ER
                edge_at[i] = G.dma(lambda e, i=i, slot=slot: e.indirect_dma_start(
                    out=edge_row[:, slot, :], out_offset=None, in_=edge_table,
                    in_offset=bass.IndirectOffsetOnAxis(ap=pick[1][:, i:i + 1], axis=0)),
                    (edge_sem[slot], 16 * (i // ER + 1)), *copied[-2:], *get(tr, t - ER // GRP),
                    *([landed_at[i - ER]] if i >= ER else []))

        def cf_nodes(t):
            for s in range(GRP):
                i = t * GRP + s
                slot = i % RING
                landed_at[i] = gather(slot, gathered[:, slot, 0:D], node_table[0],
                                      edge_row[:, i % ER, D:D + 1].bitcast(I32), edge_at[i], *table_marks,
                                      *get(msg, t - RING // GRP))

        def cf_turn(t):
            for s in range(GRP):
                i = t * GRP + s
                tr[t] = T.do(lambda e, s=s, i=i: e.transpose(bank[t % 2][:, s * P:(s + 1) * P],
                                                             edge_row[:, i % ER, 0:D], ident[:, :]),
                             edge_at[i], *get(ev, t - 2), quiet=(s < GRP - 1))

        def cf_keep(t):
            ev[t] = S.do(lambda e: e.copy(edge_t[t % 2][:, :], bank[t % 2][:, :]), tr[t], *get(hid, t - 2))

        def cf_hidden(t):
            hid[t] = T.do(lambda e: e.matmul(bank[2 + t % 2][:, :], mats["L1_gnn_We1"][:, :], edge_t[t % 2][:, :],
                                             start=True, stop=True), ev[t], *get(sp, t - 2))

        def cf_softplus(t):
            m, bk = magn[t % 2], bank[2 + t % 2]
            q0 = S.do(lambda e: e.activation(m[:, :], bk[:, :], ACT.Abs, bias=be1[:, 0:1]), hid[t], *get(sp, t - 2))
            q = S.do(lambda e: e.activation(m[:, :], m[:, :], ACT.Exp, scale=-1.0), q0)
            q = S.do(lambda e: e.activation(m[:, :], m[:, :], ACT.Ln, bias=1.0), q)
            r = V.do(lambda e: e.tensor_scalar(plus[t % 2][:, :], bk[:, :], be1[:, 0:1], 0.0, ALU.add, ALU.max),
                     q0, *get(fil, t - 2))
            sp[t] = V.do(lambda e: e.tensor_tensor(plus[t % 2][:, :], plus[t % 2][:, :], m[:, :], ALU.add), q, r)

        def cf_filter(t):
            bk = bank[4 + t % 2]
            T.do(lambda e: e.matmul(bk[:, :], ones[0:1, :], bias_fold["L1_gnn_be2"][0:1, :].unsqueeze(1)
                                    .to_broadcast([1, GRP, D]), start=True, stop=False), *get(msg, t - 2), quiet=True)
            for s in range(GRP):
                fil[t] = T.do(lambda e, s=s: e.matmul(bk[:, s * P:(s + 1) * P], plus[t % 2][:, s * P:(s + 1) * P],
                                                      mats["L1_gnn_We2"][:, :], start=False, stop=(s == GRP - 1)),
                              sp[t], quiet=(s < GRP - 1))

        def cf_message(t):
            i, s0 = t * GRP, slots(t)[0]
            msg[t] = V.do(lambda e: e.tensor_tensor(message[t % 2][:, :, :], bank[4 + t % 2][:, :]
                                                    .rearrange("p (s d) -> p s d", s=GRP),
                                                    gathered[:, s0:s0 + GRP, 0:D], ALU.mult),
                          fil[t], *landed(t), *get(po, t - 2))
            oh[t] = V.do(lambda e: e.tensor_tensor(
                hot1[t % 2][:, :, :], iota_free[:, :].unsqueeze(1).to_broadcast([P, GRP, P]),
                local[1][:, i:i + GRP].unsqueeze(2).to_broadcast([P, GRP, P]), ALU.is_equal))

        def cf_product(t):
            for s in range(GRP):
                po[t] = T.do(lambda e, s=s: e.matmul(bank[6 + t % 2][:, s * P:(s + 1) * P], hot1[t % 2][:, s, :],
                                                     message[t % 2][:, s, :], start=True, stop=True),
                             msg[t], oh[t], *get(sm, t - 2), quiet=(s < GRP - 1))

        def plain_sum(which, po, sm):
            def stage(t):
                block_registers(which, t)
                q = None
                for s in range(GRP):
                    i = t * GRP + s
                    o = bank[6 + t % 2][:, s * P:(s + 1) * P]

                    def add(e, i=i, o=o):
                        a = block_sum(e, i, D)
                        return e.tensor_tensor(a, a, o, ALU.add)
                    q = V.do(add, po[t], *([q] if q else get(sm, t - 1)))
                sm[t] = q
            return stage

        pipeline(TICKS, [cf_edges, cf_nodes, cf_turn, cf_keep, cf_hidden, cf_softplus, cf_filter, cf_message,
                         cf_product, plain_sum(1, po, sm)])
        barrier()

        first, norm = Dense(bank[0:2], bank[2:4], xt), Norm()
        sp_n, rel_n, res_n = {}, {}, {}
        third_buf = [sb_ring(f"third_buf{k}", [P, GRP * P]) for k in range(2)]
        third = Dense([bank[5]] * 2, bank[6:8], third_buf)
        m_t1 = (sem("table1_out"), 16 * NS)

        def n2_softplus(n):
            wid = len(sets[n]) * P
            m, r, bk = magn[n % 2], plus[n % 2], bank[2 + n % 2]
            col = cols["L1_gnn_b2"]
            q0 = S.do(lambda e: e.activation(m[:, 0:wid], bk[:, 0:wid], ACT.Abs, bias=col[:, 0:1]), first.mm[n],
                      *get(sp_n, n - 2))
            q = S.do(lambda e: e.activation(m[:, 0:wid], m[:, 0:wid], ACT.Exp, scale=-1.0), q0)
            q = S.do(lambda e: e.activation(m[:, 0:wid], m[:, 0:wid], ACT.Ln, bias=1.0), q)
            r0 = V.do(lambda e: e.tensor_scalar(r[:, 0:wid], bk[:, 0:wid], col[:, 0:1], 0.0, ALU.add, ALU.max),
                      q0, *get(rel_n, n - 2))
            sp_n[n] = V.do(lambda e: e.tensor_tensor(r[:, 0:wid], r[:, 0:wid], m[:, 0:wid], ALU.add), q, r0)
            first.used[n] = sp_n[n]

        def second_times(n, buf, ready, mat, bias_row, done, used):
            cnt = len(sets[n])
            T.do(lambda e: e.matmul(bank[4][:, 0:cnt * P], ones[0:1, :],
                                    bias_row[0:1, :].unsqueeze(1).to_broadcast([1, cnt, D]), start=True, stop=False),
                 *get(used, n - 1), quiet=True)
            for k in range(cnt):
                done[n] = T.do(lambda e, k=k: e.matmul(bank[4][:, k * P:(k + 1) * P], buf[n % 2][:, k * P:(k + 1) * P],
                                                       mat[:, :], start=False, stop=(k == cnt - 1)),
                               ready, quiet=(k < cnt - 1))

        def n2_res(n):
            b0, b1 = span(n)
            wid = (b1 - b0) * P
            res_n[n] = V.do(lambda e: e.scalar_tensor_tensor(
                res[n % 4][:, 0:b1 - b0, :], x_sb[:, b0:b1, :], 2.0,
                bank[4][:, 0:wid].rearrange("p (b d) -> p b d", d=D), ALU.mult, ALU.add), rel_n[n])
            norm.stats(n, res_n[n])

        def n2_rows(n):
            for k, b in enumerate(sets[n]):
                third.used[n] = S.do(lambda e, k=k, b=b: e.activation(
                    acc[:, b, 0:D], bank[6 + n % 2][:, k * P:(k + 1) * P], ACT.Copy, scale=inv_sqrt_deg[:, b:b + 1]),
                    third.mm[n], first.tr[n])
            b0, b1 = span(n)
            Y.dma(lambda e: e.dma_start(node_table[1][b0 * P:b1 * P, :].rearrange("(b p) d -> p b d", p=P),
                                        acc[:, b0:b1, 0:D]), m_t1, third.used[n])

        pipeline(NS, [lambda n: first.turn(n, lambda b: acc[:, b, 0:D]), first.keep,
                      lambda n: first.columns(n, mats["L1_gnn_W2"]), n2_softplus,
                      lambda n: second_times(n, plus, sp_n[n], mats["L1_gnn_W3"], bias_fold["L1_gnn_b3"], rel_n, res_n),
                      n2_res, norm.root, norm.scale,
                      lambda n: third.turn(n, lambda b: x_sb[:, b, :], norm.x[n], *get(third.ev, n - 1)), third.keep,
                      lambda n: third.times(n, gcn_w), n2_rows])
        barrier()

        def plain_layer(table, ready):
            oh, po, sm = {}, {}, {}

            def fetch(t):
                for s in range(GRP):
                    i = t * GRP + s
                    landed_at[i] = gather(i % RING, gathered[:, i % RING, 0:D], table, pick[0][:, i:i + 1], ready,
                                          *get(po, t - RING // GRP))

            def one_hot(t):
                i = t * GRP
                oh[t] = V.do(lambda e: e.tensor_tensor(
                    hot[t % 2][:, :, :], iota_free[:, :].unsqueeze(1).to_broadcast([P, GRP, P]),
                    local[0][:, i:i + GRP].unsqueeze(2).to_broadcast([P, GRP, P]), ALU.is_equal), *get(po, t - 2))

            def product(t):
                for s, slot in enumerate(slots(t)):
                    po[t] = T.do(lambda e, s=s, slot=slot: e.matmul(
                        bank[6 + t % 2][:, s * P:(s + 1) * P], hot[t % 2][:, s, :], gathered[:, slot, 0:D],
                        start=True, stop=True), oh[t], landed_at[t * GRP + s], *get(sm, t - 2), quiet=(s < GRP - 1))

            pipeline(TICKS, [fetch, one_hot, product, plain_sum(0, po, sm)])

        plain_layer(node_table[1], m_t1)
        barrier()

        norm = Norm()
        m_t2 = (sem("table2_out"), 16 * NS)

        def n3_res(n):
            b0, b1 = span(n)
            q = V.do(lambda e: e.tensor_tensor(xb[n % 2][:, 0:b1 - b0, :], x_sb[:, b0:b1, :],
                                               rows["L2_gnn_b"][:, :].unsqueeze(1).to_broadcast([P, b1 - b0, D]),
                                               ALU.add))
            for k, b in enumerate(sets[n]):
                p = V.do(lambda e, k=k, b=b: e.scalar_tensor_tensor(
                    res[n % 4][:, k, :], acc[:, b, 0:D], inv_sqrt_deg[:, b:b + 1], xb[n % 2][:, k, :],
                    ALU.mult, ALU.add), q)
            norm.stats(n, p)

        def n3_rows(n):
            b0, b1 = span(n)
            S.do(lambda e: e.copy(acc[:, b0:b1, 0:D], x_sb[:, b0:b1, :]), norm.x[n])
            Y.dma(lambda e: e.dma_start(node_table[2][b0 * P:b1 * P, :].rearrange("(b p) d -> p b d", p=P),
                                        x_sb[:, b0:b1, :]), m_t2, norm.x[n])

        pipeline(NS, [n3_res, norm.root, norm.scale, n3_rows])
        barrier()
        plain_layer(node_table[2], m_t2)
        barrier()

        first, norm = Dense(bank[0:2], bank[2:4], xt), Norm()
        act_n, rel_n, res_n = {}, {}, {}
        m_out = (sem("out_written"), 16 * (NS + 0))

        def n4_relu(n):
            wid = len(sets[n]) * P
            act_n[n] = S.do(lambda e: e.activation(plus[n % 2][:, 0:wid], bank[2 + n % 2][:, 0:wid], ACT.Relu,
                                                   bias=cols["L3_gnn_b1"][:, 0:1]), first.mm[n], *get(rel_n, n - 2))
            first.used[n] = act_n[n]

        def n4_res(n):
            b0, b1 = span(n)
            wid = (b1 - b0) * P
            res_n[n] = V.do(lambda e: e.tensor_tensor(
                res[n % 4][:, 0:b1 - b0, :], x_sb[:, b0:b1, :],
                bank[4][:, 0:wid].rearrange("p (b d) -> p b d", d=D), ALU.add), rel_n[n])
            norm.stats(n, res_n[n])

        def n4_store(n):
            b0, b1 = span(n)
            if b1 < NB:
                Y.dma(lambda e: e.dma_start(out[b0 * P:b1 * P, :].rearrange("(b p) d -> p b d", p=P),
                                            x_sb[:, b0:b1, :]), m_out, norm.x[n])
            else:
                assert b1 - b0 == 1
                Y.dma(lambda e: e.dma_start(out[b0 * P:N, :], x_sb[0:LAST, b0, :]), m_out, norm.x[n])

        pipeline(NS, [lambda n: first.turn(n, lambda b: acc[:, b, 0:D]), first.keep,
                      lambda n: first.columns(n, mats["L3_gnn_W1"]), n4_relu,
                      lambda n: second_times(n, plus, act_n[n], mats["L3_gnn_W2"], rows["L3_gnn_b2"], rel_n, res_n),
                      n4_res, norm.root, norm.scale, n4_store])
        Y.items.append(((m_x, m_w, m_out, m_t1, m_t2, *table_marks, *copied[-2:]), None, None))
        finish(nc, ctx, V, S, T, G, Y)


def finish(nc, ctx, V, S, T, G, Y):
    block = ctx.enter_context(nc.Block())
    block.vector(V.play)
    block.scalar(S.play)
    block.tensor(T.play)
    block.gpsimd(G.play)
    block.sync(Y.play)


INPUTS = ["x", "src", "dst", "edge_attr_128", "L0_gnn_W", "L0_gnn_att_src", "L0_gnn_att_dst", "L0_gnn_bias",
          "L1_gnn_Wn", "L1_gnn_We1", "L1_gnn_be1", "L1_gnn_We2", "L1_gnn_be2", "L1_gnn_W2", "L1_gnn_b2",
          "L1_gnn_W3", "L1_gnn_b3", "L2_gnn_W", "L2_gnn_b", "L3_gnn_W1", "L3_gnn_b1", "L3_gnn_W2", "L3_gnn_b2"]


def kernel(**inputs):
    import numpy as np
    import concourse.bacc as bacc
    from concourse.bass_utils import run_bass_kernel_spmd as run

    nc = bacc.Bacc("TRN2", target_bir_lowering=False, num_devices=1)
    arrays, args = {}, {}
    for name in INPUTS:
        arrays[name] = np.ascontiguousarray(inputs[name])
        args[name] = nc.dram_tensor(name, arrays[name].shape, mybir.dt.from_np(arrays[name].dtype),
                                    kind="ExternalInput").ap()
    out = nc.dram_tensor("out", (N, D), F32, kind="ExternalOutput").ap()
    build_program(nc, args, out)
    return run(nc, [arrays], core_ids=[0]).results[0]["out"]
```

```python
from contextlib import ExitStack

import concourse.bass as bass
from concourse import mybir

F32, BF16, I32, U32 = mybir.dt.float32, mybir.dt.bfloat16, mybir.dt.int32, mybir.dt.uint32
ALU = mybir.AluOpType
ACT = mybir.ActivationFunctionType
AX = mybir.AxisListType

P = 128
N, E, D = 6250, 100000, 128
NB = -(-N // P)
LAST = N - (NB - 1) * P
GRP = 4
STEPS = -(-(E // P + 1 + NB - 1) // GRP) * GRP
TICKS = STEPS // GRP
SG = -(-STEPS // P)
SW = SG * P
EP, EJ = 125, E // 125
LOGN = 17
PLACES = 1 << LOGN
SF = PLACES // P
LOGF = SF.bit_length() - 1
LP = -(-E // SF)
LREST = E - (LP - 1) * SF
NO_NODE = 7000
SRC_BITS, EID_BITS = 13, 17
KEY_BASE = 0x40000000
KEY_MASK = KEY_BASE - 1
PAD_KEY = 0x7F000000
SIGN = 0x80000000
BIG = float(2 ** 100)
LOG2 = 0.6931471824645996
SLOPE = 0.2
EPS = 1e-5
RING = 40
ER = RING // 2
SPAN = 16 * GRP
ARENA_WORDS = 29900
COPY_J = 10


class Line:

    def __init__(self, ctx, nc, name):
        self.ctx, self.nc, self.name, self.items, self.phase = ctx, nc, name, [], 0
        self.new_phase()

    def new_phase(self):
        self.sem = self.ctx.enter_context(self.nc.semaphore(f"{self.name}_{self.phase}"))
        self.count, self.phase = 0, self.phase + 1

    def do(self, fn, *after, quiet=False):
        self.items.append((after, fn, None if quiet else (self.sem, 1)))
        if quiet:
            return None
        self.count += 1
        return (self.sem, self.count)

    def dma(self, fn, mark, *after):
        self.items.append((after, fn, (mark[0], 16)))
        return mark

    def play(self, eng):
        self.emit(eng, self.items, {})

    def emit(self, eng, items, seen):
        for after, fn, inc in items:
            for sem, value in after:
                if seen.get(sem.name, 0) < value:
                    eng.wait_ge(sem, value)
                    seen[sem.name] = value
            if fn is None:
                continue
            if isinstance(fn, Branch):
                reg = eng.register("branch_flag").__enter__()
                eng.load(reg, fn.flag)
                with eng.If_ne(reg, 0):
                    self.emit(eng, fn.items, dict(seen))
                continue
            ins = fn(eng)
            if inc:
                ins.then_inc(*inc)


class Branch:

    def __init__(self, flag, items):
        self.flag, self.items = flag, items


def branch(lines, flag, ready, body):
    kept = []
    for l in lines:
        kept.append((l.items, l.sem, l.count))
        l.items = []
        l.new_phase()
    body()
    for l, (items, sem, count) in zip(lines, kept):
        items.append(((ready,), Branch(flag, l.items), None))
        l.items, l.sem, l.count = items, sem, count


def build_program(nc, A, out):
    with ExitStack() as ctx:
        def sb(name, shape, dt=F32):
            return ctx.enter_context(nc.sbuf_tensor(name, shape, dt))

        arena = sb("arena", [P, ARENA_WORDS])
        taken = [0]

        def sb_ring(name, shape, dt=F32):
            parts, free = shape[0], 1
            for n in shape[1:]:
                free *= n
            words = -(-free * (2 if dt == BF16 else 4) // 4)
            at = taken[0]
            taken[0] = at + words
            assert taken[0] <= ARENA_WORDS, (name, taken[0])
            view = arena[0:parts, at:at + words].bitcast(dt)[:, 0:free]
            if len(shape) == 3:
                view = view.rearrange("p (a b) -> p a b", a=shape[1])
            return view

        def dram(name, shape, dt=F32):
            return nc.dram_tensor(name, shape, dt, kind="Internal").ap()

        def sem(name):
            return ctx.enter_context(nc.semaphore(name))

        bank = [ctx.enter_context(nc.psum_tensor(f"bank{i}", [P, 512], F32)) for i in range(8)]
        V, S, T, G, Y = (Line(ctx, nc, n) for n in ("vector", "scalar", "tensor", "gpsimd", "sync"))

        def barrier(*marks):
            ends = [(l.sem, l.count) for l in (V, S, T, G) if l.count] + list(marks)
            for l in (V, S, T, G, Y):
                l.items.append((tuple(ends), None, None))
            for l in (V, S, T, G):
                l.new_phase()

        sorted_keys = [dram(f"sorted_keys{k}", [PLACES], U32) for k in range(2)]
        step_block = [dram(f"step_block{k}", [SW]) for k in range(2)]
        gat_table = dram("gat_table", [NB * P, D + 2])
        node_table = [dram(f"node_table{k}", [NB * P, D]) for k in range(3)]
        edge_table = dram("edge_table", [E, D + 1])

        iota_free = sb("iota_free", [P, P])
        iota_part = sb("iota_part", [P, 1])
        ident = sb("ident", [P, P])
        ident_bf = sb("ident_bf", [P, P], BF16)
        big_ident = sb("big_ident", [P, P], BF16)
        neg_big_row = sb("neg_big_row", [1, P], BF16)
        ones_row = sb("ones_row", [1, GRP * P], BF16)
        ones = sb("ones", [P, P])
        const_done = []

        def c(line, fn, *after):
            t = line.do(fn, *after)
            const_done.append(t)
            return t

        c_iota = c(G, lambda e: e.iota(iota_free[:, :], [[1, P]], base=0, channel_multiplier=0,
                                       allow_small_or_imprecise_dtypes=True))
        c_part = c(G, lambda e: e.iota(iota_part[:, :], [[0, 1]], base=0, channel_multiplier=1,
                                       allow_small_or_imprecise_dtypes=True))
        c_ident = c(V, lambda e: e.tensor_scalar(ident[:, :], iota_free[:, :], iota_part[:, 0:1], None, ALU.is_equal),
                    c_iota, c_part)
        c(V, lambda e: e.tensor_copy(ident_bf[:, :], ident[:, :]), c_ident)
        c(V, lambda e: e.tensor_scalar(big_ident[:, :], ident[:, :], BIG, None, ALU.mult), c_ident)
        c(V, lambda e: e.memset(neg_big_row[:, :], -BIG))
        c(V, lambda e: e.memset(ones_row[:, :], 1.0))
        c(V, lambda e: e.memset(ones[:, :], 1.0))

        x_sb = sb("x_sb", [P, NB, D])
        list_index = {k: sb_ring(f"index_{k}", [LP, SF], U32) for k in ("dst", "src")}
        m_list_index = (sem("list_index_loaded"), 16 * 4)
        for k in ("dst", "src"):
            tile, flat = list_index[k][:, :].bitcast(I32), A[k]
            z = V.do(lambda e, tile=tile: e.memset(tile, NO_NODE))
            Y.dma(lambda e, tile=tile, flat=flat: e.dma_start(
                tile[0:LP - 1, :], flat[0:(LP - 1) * SF].rearrange("(p f) -> p f", f=SF)), m_list_index, z)
            Y.dma(lambda e, tile=tile, flat=flat: e.dma_start(
                tile[LP - 1:LP, 0:LREST], flat[(LP - 1) * SF:E].rearrange("(p f) -> p f", p=1)), m_list_index, z)
        copy_dst = sb_ring("copy_dst", [EP, EJ], U32)
        m_index = (sem("copy_dst_loaded"), 16)
        Y.dma(lambda e: e.dma_start(copy_dst[:, :].bitcast(I32), A["dst"].rearrange("(p j) -> p j", p=EP)), m_index)
        z_x = V.do(lambda e: e.memset(x_sb[:, NB - 1, :], 0.0))
        m_x = (sem("x_loaded"), 32)
        full = (NB - 1) * P
        Y.dma(lambda e: e.dma_start(x_sb[:, 0:NB - 1, :], A["x"][0:full, :].rearrange("(b p) d -> p b d", p=P)), m_x)
        Y.dma(lambda e: e.dma_start(x_sb[0:LAST, NB - 1, :], A["x"][full:N, :]), m_x, z_x)
        mats = {}
        rows = {}
        m_w = (sem("weights_loaded"), 0)
        n_w = 0
        for name in ("L0_gnn_W", "L1_gnn_Wn", "L1_gnn_We1", "L1_gnn_We2", "L1_gnn_W2", "L1_gnn_W3",
                     "L2_gnn_W", "L3_gnn_W1", "L3_gnn_W2"):
            mats[name] = sb("w_" + name, [P, D])
            Y.dma(lambda e, n=name: e.dma_start(mats[n][:, :], A[n]), m_w)
            n_w += 1
        for name in ("L0_gnn_att_src", "L0_gnn_att_dst", "L0_gnn_bias", "L1_gnn_be2", "L1_gnn_b3",
                     "L2_gnn_b", "L3_gnn_b2"):
            rows[name] = sb("r_" + name, [P, D])
            Y.dma(lambda e, n=name: e.dma_start(rows[n][:, :], A[n].rearrange("(o d) -> o d", o=1)
                                                .to_broadcast([P, D])), m_w)
            n_w += 1
        cols = {}
        for name in ("L1_gnn_be1", "L1_gnn_b2", "L3_gnn_b1"):
            cols[name] = sb("c_" + name, [P, 1])
            Y.dma(lambda e, n=name: e.dma_start(cols[n][:, :], A[n].rearrange("(d o) -> d o", o=1)), m_w)
            n_w += 1
        m_w = (m_w[0], 16 * n_w)

        copy_tile = [sb_ring(f"copy_tile{i}", [EP, COPY_J, D + 1]) for i in range(2)]
        copy_in = [sem(f"copy_in{i}") for i in range(2)]
        copy_out = [sem(f"copy_out{i}") for i in range(2)]
        edges = A["edge_attr_128"].rearrange("(p j) d -> p j d", p=EP)
        edges_dst = edge_table.rearrange("(p j) d -> p j d", p=EP)
        n_copy = EJ // COPY_J

        def copy_edge_tile(n):
            i, turn, j = n % 2, n // 2, n * COPY_J
            tile = copy_tile[i]
            free = [(copy_out[i], 16 * turn)] if turn else []
            got = Y.dma(lambda e: e.dma_start(tile[:, :, 0:D], edges[:, j:j + COPY_J, :]),
                        (copy_in[i], 16 * (turn + 1)), *free)
            put = G.do(lambda e: e.tensor_copy(tile[:, :, D].bitcast(U32), copy_dst[:, j:j + COPY_J]),
                       m_index, *free)
            return got, put

        def store_edge_tile(n, got, put):
            i, turn, j = n % 2, n // 2, n * COPY_J
            return Y.dma(lambda e: e.dma_start(edges_dst[:, j:j + COPY_J, :], copy_tile[i][:, :, :]),
                         (copy_out[i], 16 * (turn + 1)), got, put)

        def copy_edges():
            loads = [copy_edge_tile(0)]
            for n in range(n_copy):
                if n + 1 < n_copy:
                    loads.append(copy_edge_tile(n + 1))
                copied.append(store_edge_tile(n, *loads[n]))
                yield

        copied = []

        gat_w = sb_ring("gat_w", [P, D + 2])
        att_prod = sb_ring("att_prod", [P, D])
        acc = sb("acc", [P, NB + 1, D + 2])
        dst_part = sb("dst_part", [P, NB + 1])
        xt = [sb(f"xt{k}", [P, GRP * P]) for k in range(2)]
        m_gat_table = (sem("gat_table_out"), 16)

        def build_gat_table():
            w0 = V.do(lambda e: e.tensor_copy(gat_w[:, 0:D], mats["L0_gnn_W"][:, :]), m_w)
            t = V.do(lambda e: e.tensor_tensor_reduce(out=att_prod[:, :], in0=mats["L0_gnn_W"][:, :],
                                                      in1=rows["L0_gnn_att_src"][:, :], scale=1.0, scalar=0.0,
                                                      op0=ALU.mult, op1=ALU.add, accum_out=gat_w[:, D:D + 1]), m_w)
            t = V.do(lambda e: e.tensor_tensor_reduce(out=att_prod[:, :], in0=mats["L0_gnn_W"][:, :],
                                                      in1=rows["L0_gnn_att_dst"][:, :], scale=1.0, scalar=0.0,
                                                      op0=ALU.mult, op1=ALU.add, accum_out=gat_w[:, D + 1:D + 2]), t)
            z = V.do(lambda e: e.memset(acc[:, NB, :], 0.0))
            z = V.do(lambda e: e.memset(acc[:, 0:NB, D:D + 1], 1.0), z)
            z = V.do(lambda e: e.memset(dst_part[:, NB:NB + 1], 0.0), z)
            sets = [list(range(b, min(b + 3, NB))) for b in range(0, NB, 3)]
            turned_x, evac, prod, kept = {}, {}, {}, {}
            for n in range(len(sets) + 1):
                if n < len(sets):
                    bs = sets[n]
                    for k, b in enumerate(bs):
                        turned_x[n] = T.do(lambda e, b=b, k=k: e.transpose(bank[5][:, k * P:(k + 1) * P], x_sb[:, b, :],
                                                                           ident[:, :]),
                                           m_x, c_ident, *([evac[n - 1]] if n else []), quiet=(k < len(bs) - 1))
                    wid = len(bs) * P
                    evac[n] = V.do(lambda e, n=n, wid=wid: e.tensor_copy(xt[n % 2][:, 0:wid], bank[5][:, 0:wid]),
                                   turned_x[n], *([prod[n - 2]] if n > 1 else []))
                if n:
                    n1 = n - 1
                    bs = sets[n1]
                    bk = bank[6 + n1 % 2]
                    for k, b in enumerate(bs):
                        prod[n1] = T.do(lambda e, k=k, n1=n1, bk=bk: e.matmul(
                            bk[:, k * (D + 2):(k + 1) * (D + 2)], xt[n1 % 2][:, k * P:(k + 1) * P], gat_w[:, :],
                            start=True, stop=True), evac[n1], w0, t, *([kept[n1 - 2]] if n1 > 1 else []),
                            quiet=(k < len(bs) - 1))
                    v = bk[:, 0:len(bs) * (D + 2)].rearrange("p (b d) -> p b d", d=D + 2)
                    b0, b1 = bs[0], bs[-1] + 1
                    V.do(lambda e, v=v, b0=b0, b1=b1: e.tensor_copy(acc[:, b0:b1, 0:D], v[:, :, 0:D]), prod[n1], z,
                         quiet=True)
                    V.do(lambda e, v=v, b0=b0, b1=b1: e.tensor_copy(acc[:, b0:b1, D + 1], v[:, :, D]), quiet=True)
                    kept[n1] = V.do(lambda e, v=v, b0=b0, b1=b1: e.tensor_copy(dst_part[:, b0:b1], v[:, :, D + 1]))
            Y.dma(lambda e: e.dma_start(gat_table.rearrange("(b p) d -> p b d", p=P), acc[:, 0:NB, :]),
                  m_gat_table, kept[len(sets) - 1], z)

        place = sb_ring("place", [P, SF], U32)
        place_x = sb_ring("place_x", [P, SF], U32)
        c_place = c(G, lambda e: e.iota(place[:, :], [[1, SF]], base=0, channel_multiplier=SF))
        sh = V.do(lambda e: e.tensor_scalar(place_x[:, :], place[:, :], 1, None, ALU.logical_shift_left), c_place)
        c_px = V.do(lambda e: e.tensor_tensor(place_x[:, :], place_x[:, :], place[:, :], ALU.bitwise_xor), sh)
        keys = [sb_ring(f"keys{i}", [P, SF], U32) for i in range(2)]
        flip = sb_ring("flip", [P, SF], U32)

        def make_keys(hi, lo, lo_bits, after):
            t = V.do(lambda e: e.memset(keys[0][:, :].bitcast(I32), PAD_KEY), *after)
            k0 = keys[0][0:LP, :]
            t = V.do(lambda e: e.tensor_scalar(k0, hi[:, :], lo_bits, KEY_BASE, ALU.logical_shift_left, ALU.bitwise_or),
                     t, m_list_index)
            return V.do(lambda e: e.tensor_tensor(k0, k0, lo, ALU.bitwise_or), t, c_place)

        def turn_over(src, dst, after):
            v = after
            for h in range(2):
                for q in range(4 * h, 4 * h + 4):
                    t = T.do(lambda e, q=q: e.transpose(bank[3][:, (q % 4) * P:(q % 4 + 1) * P],
                                                        src[:, q * P:(q + 1) * P].bitcast(F32), ident[:, :]),
                             v, c_ident, quiet=(q % 4 != 3))
                v = S.do(lambda e, h=h: e.copy(dst[:, 512 * h:512 * h + 512].bitcast(F32), bank[3][:, :]), t)
            return v

        def sort_keys(t):
            cur = 0
            for k in range(1, LOGN + 1):
                base = place if k == 1 else place_x
                f = V.do(lambda e, k=k, base=base: e.tensor_scalar(
                    flip[:, :], base[:, :], 31 - k, SIGN, ALU.logical_shift_left, ALU.bitwise_and), t, c_px)
                yield
                t = V.do(lambda e, cur=cur: e.tensor_tensor(keys[1 - cur][:, :], keys[cur][:, :], flip[:, :],
                                                            ALU.bitwise_xor), f)
                cur = 1 - cur
                yield
                distances = [1 << j for j in reversed(range(min(k, LOGF)))]
                if k > LOGF:
                    distances = [-(1 << j) for j in reversed(range(k - LOGF))] + distances
                over = False
                for d in distances:
                    if (d < 0) != over:
                        t = turn_over(keys[cur], keys[1 - cur], t)
                        cur, over = 1 - cur, d < 0
                        yield
                    a = keys[cur][:, :].bitcast(F32).rearrange("p (n two m) -> p n two m", two=2, m=abs(d))
                    b = keys[1 - cur][:, :].bitcast(F32).rearrange("p (n two m) -> p n two m", two=2, m=abs(d))
                    V.do(lambda e, a=a, b=b: e.tensor_tensor(b[:, :, 0, :], a[:, :, 0, :], a[:, :, 1, :], ALU.min),
                         t, quiet=True)
                    t = V.do(lambda e, a=a, b=b: e.tensor_tensor(b[:, :, 1, :], a[:, :, 0, :], a[:, :, 1, :], ALU.max), t)
                    cur = 1 - cur
                    yield
            assert cur == 0
            sorted_at.append(t)

        sorted_at = []

        off_bias = sb_ring("off_bias", [P, NB + 1])
        c_ob = c(G, lambda e: e.iota(off_bias[:, :], [[-P, NB + 1]], base=0, channel_multiplier=0,
                                     allow_small_or_imprecise_dtypes=True))
        c_ob = V.do(lambda e: e.tensor_scalar(off_bias[:, :], off_bias[:, :], 0.5, None, ALU.add), c_ob)
        step_no = sb_ring("step_no", [P, SG])
        c_sn = c(G, lambda e: e.iota(step_no[:, :], [[P, SG]], base=0, channel_multiplier=1,
                                     allow_small_or_imprecise_dtypes=True))
        sign_junk = sb_ring("sign_junk", [LP, SF], BF16)
        below = [sb_ring(f"below{k}", [LP, NB + 1]) for k in range(2)]
        offset = sb_ring("offset", [P, NB + 1])
        count = sb_ring("count", [P, NB])
        chunks_i = sb_ring("chunks_i", [P, NB], I32)
        chunks = sb_ring("chunks", [P, NB])
        zeros = sb("zeros", [P, NB + 1])
        c_z = c(V, lambda e: e.memset(zeros[:, :], 0.0))
        chunk_end = sb_ring("chunk_end", [P, NB])
        slack = sb_ring("slack", [P, NB])
        passed = sb_ring("passed", [P, SG, NB])
        passed_w = sb_ring("passed_w", [P, SG, NB])
        blk_col = [sb(f"blk_col{k}", [P, SG]) for k in range(2)]
        start_f = sb_ring("start_f", [P, SG])
        start_u = sb_ring("start_u", [P, SG], U32)
        window = sb_ring("window", [P, SW], U32)
        win_part = flip[:, 0:SW]
        win_f = sb_ring("win_f", [P, SW])
        blk_row = [sb_ring(f"blk_row{k}", [P, SW]) for k in range(2)]
        blk_ints = sb("blk_ints", [33, SW], I32)
        blk_int = [blk_ints[32 * k:32 * k + 1, :] for k in range(2)]
        local = [sb(f"local{k}", [P, SW]) for k in range(2)]
        pick = [sb(f"pick{k}", [P, SW], I32) for k in range(2)]

        def count_below(i, index):
            a = V.do(lambda e: e.memset(below[i][:, 0:1], float(SF)))
            for b in range(1, NB + 1):
                a = S.do(lambda e, b=b: e.activation(sign_junk[:, :], index[:, :], ACT.Sign,
                                                     bias=off_bias[0:LP, b:b + 1], accum_out=below[i][:, b:b + 1]),
                         c_ob, a, m_list_index)
                yield
            counted.append(a)

        counted = []

        def step_table(i, lo_bits, rows_of_table, list_sorted, list_ready, Q):
            blk = blk_col[i]
            mm = T.do(lambda e: e.matmul(bank[3][:, 0:NB + 1], ones[0:LP, :], below[i][:, :], start=True, stop=True),
                      counted[i], list_sorted, *const_done)
            yield
            t = V.do(lambda e: e.tensor_scalar(offset[:, :], bank[3][:, 0:NB + 1], -0.5, float(LP * SF) / 2,
                                               ALU.mult, ALU.add), mm, *table_used)
            t = V.do(lambda e: e.tensor_tensor(count[:, :], offset[:, 1:NB + 1], offset[:, 0:NB], ALU.subtract), t)
            u = V.do(lambda e: e.tensor_scalar(chunks_i[:, :], count[:, :], float(P - 1), None, ALU.add), t)
            u = V.do(lambda e: e.tensor_scalar(chunks_i[:, :], chunks_i[:, :], 7, None, ALU.logical_shift_right), u)
            u = V.do(lambda e: e.tensor_copy(chunks[:, :], chunks_i[:, :]), u)
            w = V.do(lambda e: e.scalar_tensor_tensor(slack[:, :], chunks[:, :], -float(P), count[:, :],
                                                      ALU.mult, ALU.add), u)
            w = V.do(lambda e: e.tensor_tensor_scan(chunk_end[:, :], chunks[:, :], zeros[:, 0:NB], 0.0,
                                                    ALU.add, ALU.add), u, c_z)
            w = V.do(lambda e: e.tensor_tensor(passed[:, :, :], chunk_end[:, :].unsqueeze(1).to_broadcast([P, SG, NB]),
                                               step_no[:, :].unsqueeze(2).to_broadcast([P, SG, NB]), ALU.is_le),
                     w, c_sn)
            r = V.do(lambda e: e.tensor_reduce(blk[:, :], passed[:, :, :], AX.X, ALU.add), w)
            w = V.do(lambda e: e.tensor_tensor(passed_w[:, :, :], passed[:, :, :],
                                               slack[:, :].unsqueeze(1).to_broadcast([P, SG, NB]), ALU.mult), w)
            w = V.do(lambda e: e.tensor_reduce(start_f[:, :], passed_w[:, :, :], AX.X, ALU.add), w)
            w = V.do(lambda e: e.scalar_tensor_tensor(start_u[:, :], step_no[:, :], float(P), start_f[:, :],
                                                      ALU.mult, ALU.add), w)
            m1 = Q.dma(lambda e: e.dma_start(step_block[i].rearrange("(g p) -> p g", p=P), blk[:, :],
                                             allow_slow_non_contiguous=True), (sem(f"blk_out{i}"), 16), r)
            m2 = Q.dma(lambda e: e.dma_start(blk_row[i][:, :], step_block[i].rearrange("(o s) -> o s", o=1)
                                             .to_broadcast([P, SW])), (sem(f"blk_in{i}"), 16), m1)
            m3 = (sem(f"windows{i}"), 16 * SG)
            for _ in range(8):
                yield
            for g in range(SG):
                G.dma(lambda e, g=g: e.indirect_dma_start(
                    out=window[:, g * P:(g + 1) * P], out_offset=None,
                    in_=sorted_keys[i].rearrange("(n o) -> n o", o=1),
                    in_offset=bass.IndirectOffsetOnAxis(ap=start_u[:, g:g + 1], axis=0)), m3, w, list_ready,
                    *table_used)
            yield
            bi = V.do(lambda e: e.tensor_copy(blk_int[i], blk_row[i][32 * i:32 * i + 1, :]), m2)
            last, got = list(table_used), []
            for part in range(2):
                if part == 0:
                    q = V.do(lambda e: e.tensor_scalar(win_part[:, :], window[:, :], KEY_MASK, lo_bits,
                                                       ALU.bitwise_and, ALU.logical_shift_right), m3, *last)
                else:
                    q = V.do(lambda e: e.tensor_scalar(win_part[:, :], window[:, :], (1 << lo_bits) - 1, None,
                                                       ALU.bitwise_and), m3, *last)
                yield
                q = V.do(lambda e: e.tensor_copy(win_f[:, :], win_part[:, :]), q, *last)
                yield
                for h in range(2):
                    lo, hi = h * 512, min((h + 1) * 512, SW)
                    for g in range(lo // P, hi // P):
                        q2 = T.do(lambda e, g=g: e.transpose(bank[3][:, (g % 4) * P:(g % 4 + 1) * P],
                                                             win_f[:, g * P:(g + 1) * P], ident[:, :]), q)
                    if part == 0:
                        q = V.do(lambda e, lo=lo, hi=hi: e.scalar_tensor_tensor(
                            local[i][:, lo:hi], blk_row[i][:, lo:hi], -float(P), bank[3][:, 0:hi - lo],
                            ALU.mult, ALU.add), q2, m2)
                    else:
                        q = V.do(lambda e, lo=lo, hi=hi: e.tensor_scalar(
                            pick[i][:, lo:hi], bank[3][:, 0:hi - lo], float(rows_of_table - 1), None, ALU.min), q2)
                    got.append(q)
                    yield
                last = [q]
            table_used[:] = last + [bi]

        table_used = []

        def run(generator):
            for _ in generator:
                pass

        ahead = keys[1][0:LP, :]
        z = V.do(lambda e: e.memset(ahead.bitcast(I32), NO_NODE))
        m_ahead = (sem("ahead_loaded"), 32)
        Y.dma(lambda e: e.dma_start(ahead[0:LP - 1, :].bitcast(I32),
                                    A["dst"][1:(LP - 1) * SF + 1].rearrange("(p f) -> p f", f=SF)), m_ahead, z)
        Y.dma(lambda e: e.dma_start(ahead[LP - 1:LP, 0:LREST - 1].bitcast(I32),
                                    A["dst"][(LP - 1) * SF + 1:E].rearrange("(p f) -> p f", p=1)), m_ahead, z)
        descents = sb("descents", [LP, 1])
        unsorted = sb("unsorted", [1, 1], I32)
        q = V.do(lambda e: e.tensor_tensor(flip[0:LP, :].bitcast(F32), list_index["dst"][:, :], ahead, ALU.is_gt),
                 m_ahead, m_list_index)
        q = V.do(lambda e: e.tensor_reduce(descents[:, :], flip[0:LP, :].bitcast(F32), AX.X, ALU.add), q)
        u = T.do(lambda e: e.matmul(bank[3][0:1, 0:1], descents[:, :], ones[0:LP, 0:1], start=True, stop=True),
                 q, *const_done)
        v_flag = V.do(lambda e: e.tensor_scalar(unsorted[:, :], bank[3][0:1, 0:1], 0.0, None, ALU.add), u)
        v_keys = make_keys(list_index["dst"], list_index["src"][:, :], SRC_BITS, [v_flag])
        run(count_below(0, list_index["dst"]))
        build_gat_table()
        branch((V, T, S), unsorted[:, :], v_keys, lambda: run(sort_keys(v_keys)))
        v_list = V.do(lambda e: e.tensor_copy(descents[:, :], descents[:, :]), v_keys)
        l1 = Y.dma(lambda e: e.dma_start(sorted_keys[0].rearrange("(p f) -> p f", p=P), keys[0][:, :]),
                   (sem("list0"), 16), v_list)
        run(step_table(0, SRC_BITS, NB * P, v_list, l1, S))
        barrier(m_list_index)

        slot_sem = [sem(f"slot{k}") for k in range(RING)]
        slot_uses = [0] * RING
        gathered = sb_ring("gathered", [P, RING, D + 2])
        hot = [sb_ring(f"hot{k}", [P, GRP, P]) for k in range(2)]
        block_regs = []

        def gather(slot, dst, table, index, *after):
            slot_uses[slot] += 1
            return G.dma(lambda e: e.indirect_dma_start(
                out=dst, out_offset=None, in_=table, in_offset=bass.IndirectOffsetOnAxis(ap=index, axis=0)),
                (slot_sem[slot], 16 * slot_uses[slot]), *after)

        def block_registers(which, tick):
            if tick % 4:
                return

            def load(e):
                if not block_regs:
                    block_regs.extend(e.register(f"block_reg{k}").__enter__() for k in range(16))
                i = tick * GRP
                return e.load(block_regs, blk_int[which][:, i:i + 16])
            V.do(load, quiet=True)

        def block_sum(e, i, width):
            b = e.snap(block_regs[i % 16], min_val=0, max_val=NB)
            return acc[:, bass.ds(b, 1), 0:width].rearrange("p o d -> p (o d)")

        def pipeline(n, stages, background=()):
            background = list(background)
            for t in range(n + max(s[0] for s in stages)):
                live = [fn(t - lag) for lag, fn, woven in stages if woven and 0 <= t - lag < n]
                left = [turns(t) for _, turns in background]
                turn = 0
                while live or any(left):
                    live = [g for g in live if next(g, "end") != "end"]
                    turn += 1
                    for k, (gen, _) in enumerate(background):
                        if left[k] and (turn % 3 == 1 or not live):
                            left[k] -= 1
                            next(gen, None)
                for lag, fn, woven in stages:
                    if not woven and 0 <= t - lag < n:
                        fn(t - lag)
            for gen, _ in background:
                for _ in gen:
                    pass

        def lagged(fns):
            return [(k, fns[k], False) for k in reversed(range(len(fns)))]

        degree_part = sb_ring("degree_part", [P, SW])
        a_dst = sb_ring("a_dst", [P, SW])
        parts = sb_ring("parts", [P, 6, SPAN + 1]).rearrange("p (k a) w -> p k a w", a=2)
        upper = parts.bitcast(BF16).rearrange("p k a (w two) -> p k a w two", two=2)[:, :, :, :, 1]
        self_max = sb_ring("self_max", [P, SW])
        same = sb_ring("same", [P, SW])
        block_hot = window[0:NB + 1, :].bitcast(F32)
        self_logit = sb("self_logit", [P, NB + 1])
        self_tmp = sb("self_tmp", [P, NB + 1])
        part_t = sb_ring("part_t", [NB + 1, 2, P])

        t = V.do(lambda e: e.tensor_copy(self_tmp[:, NB:NB + 1], zeros[:, 0:1]))
        t = V.do(lambda e: e.tensor_tensor(self_tmp[:, 0:NB], acc[:, 0:NB, D + 1], dst_part[:, 0:NB], ALU.add), t)
        t = V.do(lambda e: e.scalar_tensor_tensor(self_logit[:, :], self_tmp[:, :], SLOPE, self_tmp[:, :],
                                                  ALU.mult, ALU.max), t)
        h = V.do(lambda e: e.tensor_scalar(block_hot[:, :], blk_row[0][0:NB + 1, :], iota_part[0:NB + 1, 0:1], None,
                                           ALU.is_equal), t)
        T.do(lambda e: e.transpose(bank[0][0:NB + 1, 0:P], dst_part[:, :], ident[:, :]), quiet=True)
        u = T.do(lambda e: e.transpose(bank[0][0:NB + 1, P:2 * P], self_logit[:, :], ident[:, :]), t)
        v = V.do(lambda e: e.tensor_copy(part_t[:, :, :], bank[0][0:NB + 1, 0:2 * P]
                                         .rearrange("p (a n) -> p a n", a=2)), u)
        half = SW // 2
        for a in range(2):
            for q in range(2):
                u = T.do(lambda e, a=a, q=q: e.matmul(bank[1 + 2 * a + q][:, 0:half], part_t[:, a, :],
                                                      block_hot[:, q * half:(q + 1) * half], start=True, stop=True), v, h)
        V.do(lambda e: e.memset(parts[:, 0, 1, 0:1], 0.0), quiet=True)
        for q in range(2):
            V.do(lambda e, q=q: e.tensor_copy(a_dst[:, q * half:(q + 1) * half], bank[1 + q][:, 0:half]),
                 u, quiet=True)
            V.do(lambda e, q=q: e.tensor_copy(self_max[:, q * half:(q + 1) * half], bank[3 + q][:, 0:half]), quiet=True)
        V.do(lambda e: e.memset(degree_part[:, :], 0.0), quiet=True)
        w = V.do(lambda e: e.memset(same[:, 0:1], 0.0))
        w = V.do(lambda e: e.tensor_tensor(same[:, 1:SW], blk_row[0][:, 1:SW], blk_row[0][:, 0:SW - 1], ALU.is_equal), w)
        V.do(lambda e: e.tensor_scalar(same[:, :], same[:, :], 1.0, 1e30, ALU.subtract, ALU.mult), w)
        barrier()

        HR = 6
        hot_bf = [sb_ring(f"hot_bf{k}", [P, GRP, P], BF16) for k in range(HR)]
        hot_t = [sb_ring(f"hot_t{k}", [P, GRP, P], BF16) for k in range(3)]
        small = {n: sb("s_" + n, [P, 4, GRP]) for n in
                 ("top", "logit", "new", "old", "drop", "edge", "edge2", "weight", "scale")}

        joined = [sb(f"joined{k}", [P, GRP, 2]) for k in range(2)]
        oh, tr, msk, evc, mx, drp, pc, ez, wt, scl, hw, po, sm, adp, prt, jn = ({} for _ in range(16))

        def slots(t):
            return [(t * GRP + s) % RING for s in range(GRP)]

        def landed(t):
            return [landed_at[t * GRP + s] for s in range(GRP)]

        landed_at = {}

        def get(d, t):
            return [d[t]] if t in d else []

        def gat_gather(t):
            for s, slot in enumerate(slots(t)):
                i = t * GRP + s
                landed_at[i] = gather(slot, gathered[:, slot, :], gat_table, pick[0][:, i:i + 1],
                                      m_gat_table, *get(po, t - RING // GRP))

        def gat_hot(t):
            i = t * GRP
            oh[t] = V.do(lambda e: e.tensor_tensor(
                hot_bf[t % HR][:, :, :], iota_free[:, :].unsqueeze(1).to_broadcast([P, GRP, P]),
                local[0][:, i:i + GRP].unsqueeze(2).to_broadcast([P, GRP, P]), ALU.is_equal), *get(hw, t - HR))
            yield

        def gat_mask(t):
            for s in range(GRP):
                tr[t] = T.do(lambda e, s=s: e.transpose(bank[0][:, :].bitcast(BF16)[:, s * P:(s + 1) * P],
                                                        hot_bf[t % HR][:, s, :], ident_bf[:, :]),
                             oh[t], *get(evc, t - 1), quiet=(s < GRP - 1))
            bk = bank[2]
            T.do(lambda e: e.matmul(bk[:, :], neg_big_row[:, :], ones_row[:, :], start=True, stop=False),
                 *get(mx, t - 1), quiet=True)
            for s, slot in enumerate(slots(t)):
                o = bk[:, s * P:(s + 1) * P]
                T.do(lambda e, s=s, o=o: e.matmul(o, hot_bf[t % HR][:, s, :], big_ident[:, :], start=False, stop=False),
                     quiet=True)
                msk[t] = T.do(lambda e, s=s, o=o, slot=slot: e.matmul(
                    o, gathered[:, slot, D + 1:D + 2].to_broadcast([P, P]), ident[:, :], start=False, stop=(s == GRP - 1)),
                    landed_at[t * GRP + s], quiet=(s < GRP - 1))

        def gat_dst(t):
            i, c = t * GRP, t * GRP % SPAN
            adp[t] = S.do(lambda e: e.copy(parts[:, 0, 0, c + 1:c + 1 + GRP], a_dst[:, i:i + GRP]),
                          *get(pc, t - SPAN // GRP))

        def gat_keep(t):
            i = t * GRP
            for s in range(GRP):
                evc[t] = S.do(lambda e, s=s: e.activation(hot_t[t % 3][:, s, :], bank[0][:, :].bitcast(BF16)
                                                          [:, s * P:(s + 1) * P], ACT.Copy,
                                                          accum_out=degree_part[:, i + s:i + s + 1]),
                              tr[t], *get(pc, t - 3), quiet=(s < GRP - 1))

        def gat_max(t):
            i, r = t * GRP, t % 4
            top, logit, new, old, drop = (small[n][:, r, :] for n in ("top", "logit", "new", "old", "drop"))
            c = i % SPAN
            before, run = parts[:, 0, 1, c:c + GRP], parts[:, 0, 1, c + 1:c + 1 + GRP]
            if t and c == 0:
                V.do(lambda e: e.tensor_copy(parts[:, 0, 1, 0:1], parts[:, 0, 1, SPAN:SPAN + 1]), drp[t - 1])
            mx[t] = V.do(lambda e: e.tensor_reduce(top, bank[2][:, :].rearrange("p (s n) -> p s n", s=GRP),
                                                   AX.X, ALU.max), msk[t])
            yield
            q = V.do(lambda e: e.tensor_tensor(logit, top, a_dst[:, i:i + GRP], ALU.add), mx[t])
            yield
            q = V.do(lambda e: e.scalar_tensor_tensor(new, logit, SLOPE, logit, ALU.mult, ALU.max), q)
            yield
            q = V.do(lambda e: e.tensor_tensor(new, new, self_max[:, i:i + GRP], ALU.max), q)
            yield
            q = V.do(lambda e: e.tensor_tensor_scan(run, same[:, i:i + GRP], new, before[:, 0:1],
                                                    ALU.add, ALU.max), q, *get(pc, t - SPAN // GRP))
            yield
            for k in range(2):
                p = V.do(lambda e, k=k: e.tensor_tensor(parts[:, k + 1, :, c + 1:c + 1 + GRP],
                                                        parts[:, k, :, c + 1:c + 1 + GRP],
                                                        upper[:, k, :, c + 1:c + 1 + GRP], ALU.subtract),
                         p if k else q, adp[t])
                if k == 0:
                    yield
            prt[t] = p
            yield
            q = V.do(lambda e: e.tensor_tensor(old, before, same[:, i:i + GRP], ALU.add), q)
            yield
            q = V.do(lambda e: e.tensor_tensor(old, old, self_max[:, i:i + GRP], ALU.max), q)
            yield
            drp[t] = V.do(lambda e: e.tensor_tensor(drop, old, run, ALU.subtract), q, *get(scl, t - 4))
            yield

        def gat_pair(t):
            for s in range(GRP):
                c = (t * GRP + s) % SPAN + 1
                o = bank[1][:, 6 * s:6 * s + 6].rearrange("p (k a) -> p k a", a=2)
                pc[t] = T.do(lambda e, s=s, c=c, o=o: e.matmul(o, hot_t[t % 3][:, s, :], upper[:, :, :, c],
                                                               start=True, stop=True),
                             evc[t], prt[t], *get(jn, t - 1), quiet=(s < GRP - 1))

        def gat_logit(t):
            r, s0 = t % 4, slots(t)[0]
            edge, edge2 = (small[n][:, r, :] for n in ("edge", "edge2"))
            both = joined[t % 2][:, :, :]
            jn[t] = V.do(lambda e: e.tensor_reduce(both, bank[1][:, 0:6 * GRP].rearrange("p (s k a) -> p s a k", k=3, a=2),
                                                   AX.X, ALU.add), pc[t])
            yield
            q = V.do(lambda e: e.tensor_tensor(edge, both[:, :, 0], gathered[:, s0:s0 + GRP, D + 1], ALU.add),
                     jn[t], *landed(t))
            yield
            q = V.do(lambda e: e.scalar_tensor_tensor(edge2, edge, SLOPE, edge, ALU.mult, ALU.max), q, *get(wt, t - 4))
            yield
            ez[t] = V.do(lambda e: e.tensor_tensor(edge2, edge2, both[:, :, 1], ALU.subtract), q)
            yield

        def gat_weight(t):
            r = t % 4
            weight, edge2 = small["weight"][:, r, :], small["edge2"][:, r, :]
            q = S.do(lambda e: e.activation(edge2, edge2, ACT.Relu, scale=-1.0), ez[t])
            wt[t] = S.do(lambda e: e.activation(weight, edge2, ACT.Exp, scale=-1.0), q, *get(hw, t - 4))
            scl[t] = S.do(lambda e: e.activation(small["scale"][:, r, :], small["drop"][:, r, :], ACT.Exp),
                          drp[t], *get(sm, t - 4))
            for s in range(GRP):
                hw[t] = S.do(lambda e, s=s: e.activation(hot[t % 2][:, s, :], hot_bf[t % HR][:, s, :], ACT.Copy,
                                                         scale=weight[:, s:s + 1]),
                             wt[t], *get(po, t - 2), quiet=(s < GRP - 1))

        def sum_place(t, s):
            return bank[4 + 2 * (t % 2) + s // 3][:, (s % 3) * (D + 2):(s % 3) * (D + 2) + D + 1]

        def gat_product(t):
            for s, slot in enumerate(slots(t)):
                o = sum_place(t, s)
                po[t] = T.do(lambda e, s=s, slot=slot, o=o: e.matmul(o, hot[t % 2][:, s, :], gathered[:, slot, 0:D + 1],
                                                                     start=True, stop=True),
                             hw[t], *landed(t), *get(sm, t - 2), quiet=(s < GRP - 1))

        def gat_sum(t):
            block_registers(0, t)
            q = None
            for s in range(GRP):
                i = t * GRP + s
                o = sum_place(t, s)

                def add(e, i=i, o=o, s=s):
                    a = block_sum(e, i, D + 1)
                    return e.scalar_tensor_tensor(a, a, small["scale"][:, t % 4, s:s + 1], o, ALU.mult, ALU.add)
                q = V.do(add, po[t], scl[t], *([q] if q else get(sm, t - 1)))
                yield
            sm[t] = q


        def second_list():
            yield from sort_keys(make_keys(list_index["src"], place[0:LP, :], EID_BITS, []))
            l2 = Y.dma(lambda e: e.dma_start(sorted_keys[1].rearrange("(p f) -> p f", p=P), keys[0][:, :]),
                       (sem("list1"), 16), sorted_at[-1])
            yield from step_table(1, EID_BITS, E, sorted_at[-1], l2, Y)

        pipeline(TICKS, [(3, gat_max, True), (8, gat_sum, True), (5, gat_logit, True), (1, gat_hot, True),
                         (0, gat_gather, False), (1, gat_dst, False), (3, gat_keep, False), (6, gat_weight, False),
                         (7, gat_product, False), (4, gat_pair, False), (2, gat_mask, False)],
                 [(count_below(1, list_index["src"]), lambda t: 1), (copy_edges(), lambda t: 1),
                  (second_list(), lambda t: 1 + (t % 5 == 0))])
        barrier(*copied[-2:])
        taken[0] = 0

        sets = [list(range(b, min(b + GRP, NB))) for b in range(0, NB, GRP)]
        NS = len(sets)
        res = [sb_ring(f"res{k}", [P, GRP, D]) for k in range(4)]
        xb = [sb_ring(f"xb{k}", [P, GRP, D]) for k in range(2)]
        stats = sb("stats", [P, NB, 6])
        moments = sb("moments", [P, NB, 2])
        shift = sb("shift", [P, NB])
        rstd = sb("rstd", [P, NB])
        eps_col = sb("eps_col", [P, 1])
        w_eps = V.do(lambda e: e.memset(eps_col[:, :], EPS))

        def span(n):
            return sets[n][0], sets[n][-1] + 1

        class Norm:

            def __init__(self, logs=False):
                self.mean, self.std, self.rs, self.x, self.logs = {}, {}, {}, {}, logs

            def stats(self, n, after):
                for k, b in enumerate(sets[n]):
                    p = V.do(lambda e, k=k, b=b: e.bn_stats(stats[:, b, :], res[n % 4][:, k, :]), after)
                for b in sets[n]:
                    self.mean[n] = V.do(lambda e, b=b: e.bn_aggr(moments[:, b, :], stats[:, b, :]), p)

            def root(self, n):
                b0, b1 = span(n)
                if self.logs:
                    q = S.do(lambda e: e.activation(rstd[:, b0:b1], moments[:, b0:b1, 1], ACT.Ln,
                                                    bias=eps_col[:, 0:1]), self.mean[n], w_eps)
                    self.rs[n] = S.do(lambda e: e.activation(rstd[:, b0:b1], rstd[:, b0:b1], ACT.Exp, scale=-0.5), q)
                    return
                self.std[n] = S.do(lambda e: e.activation(rstd[:, b0:b1], moments[:, b0:b1, 1], ACT.Sqrt,
                                                          bias=eps_col[:, 0:1]), self.mean[n], w_eps)

            def invert(self, n):
                b0, b1 = span(n)
                q = V.do(lambda e: e.reciprocal(rstd[:, b0:b1], rstd[:, b0:b1]), self.std[n])
                self.rs[n] = V.do(lambda e: e.scalar_tensor_tensor(shift[:, b0:b1], moments[:, b0:b1, 0], -1.0,
                                                                   rstd[:, b0:b1], ALU.mult, ALU.mult), q)

            def scale(self, n):
                for k, b in enumerate(sets[n]):
                    quiet = k < len(sets[n]) - 1
                    if self.logs:
                        self.x[n] = V.do(lambda e, k=k, b=b: e.tensor_scalar(
                            x_sb[:, b, :], res[n % 4][:, k, :], moments[:, b, 0:1], rstd[:, b:b + 1],
                            ALU.subtract, ALU.mult), self.rs[n], quiet=quiet)
                    else:
                        self.x[n] = S.do(lambda e, k=k, b=b: e.activation(
                            x_sb[:, b, :], res[n % 4][:, k, :], ACT.Identity, scale=rstd[:, b:b + 1],
                            bias=shift[:, b:b + 1]), self.rs[n], quiet=quiet)

        class Dense:

            def __init__(self, bank_t, bank_o, buf):
                self.bt, self.bo, self.buf, self.tr, self.ev, self.mm, self.used = bank_t, bank_o, buf, {}, {}, {}, {}

            def turn(self, n, src, *after):
                for k, b in enumerate(sets[n]):
                    self.tr[n] = T.do(lambda e, k=k, b=b: e.transpose(self.bt[n % 2][:, k * P:(k + 1) * P], src(b),
                                                                      ident[:, :]),
                                      *after, *get(self.ev, n - 2), quiet=(k < len(sets[n]) - 1))

            def keep(self, n):
                wid = len(sets[n]) * P
                self.ev[n] = S.do(lambda e: e.copy(self.buf[n % 2][:, 0:wid], self.bt[n % 2][:, 0:wid]),
                                  self.tr[n], *get(self.mm, n - 2))

            def times(self, n, mat, bias_row=None):
                bk = self.bo[n % 2]
                cnt = len(sets[n])
                if bias_row is not None:
                    T.do(lambda e: e.matmul(bk[:, 0:cnt * P], ones[0:1, :],
                                            bias_row[0:1, :].unsqueeze(1).to_broadcast([1, cnt, D]),
                                            start=True, stop=False), *get(self.used, n - 2), quiet=True)
                for k in range(cnt):
                    self.mm[n] = T.do(lambda e, k=k: e.matmul(
                        bk[:, k * P:(k + 1) * P], self.buf[n % 2][:, k * P:(k + 1) * P], mat[:, :],
                        start=bias_row is None, stop=(bias_row is None or k == cnt - 1)),
                        self.ev[n], *get(self.used, n - 2), quiet=(k < cnt - 1))

            def columns(self, n, mat):
                wid = len(sets[n]) * P
                self.mm[n] = T.do(lambda e: e.matmul(self.bo[n % 2][:, 0:wid], mat[:, :], self.buf[n % 2][:, 0:wid],
                                                     start=True, stop=True), self.ev[n], *get(self.used, n - 2))

        inv_den = sb("inv_den", [P, NB])
        q = V.do(lambda e: e.tensor_scalar(inv_den[:, :], acc[:, 0:NB, D], 1e-16, None, ALU.add))
        v_den = V.do(lambda e: e.reciprocal(inv_den[:, :], inv_den[:, :]), q)
        deg_t = sb_ring("deg_t", [P, SG, P])
        group_hot = sb_ring("group_hot", [P, SG, NB])
        inv_sqrt_deg = sb("inv_sqrt_deg", [P, NB])
        for g in range(SG):
            u = T.do(lambda e, g=g: e.transpose(bank[g // 4][:, (g % 4) * P:(g % 4 + 1) * P],
                                                degree_part[:, g * P:(g + 1) * P], ident[:, :]))
        V.do(lambda e: e.tensor_copy(deg_t[:, 0:4, :], bank[0][:, :].rearrange("p (g n) -> p g n", n=P)), u, quiet=True)
        V.do(lambda e: e.tensor_copy(deg_t[:, 4:SG, :], bank[1][:, 0:(SG - 4) * P].rearrange("p (g n) -> p g n", n=P)),
             quiet=True)
        q = V.do(lambda e: e.tensor_tensor(group_hot[:, :, :], blk_col[0][:, :].unsqueeze(2).to_broadcast([P, SG, NB]),
                                           iota_free[:, 0:NB].unsqueeze(1).to_broadcast([P, SG, NB]), ALU.is_equal))
        for g in range(SG):
            u = T.do(lambda e, g=g: e.matmul(bank[2][:, 0:NB], deg_t[:, g, :], group_hot[:, g, :], start=(g == 0),
                                             stop=(g == SG - 1)), q)
        q = S.do(lambda e: e.activation(inv_sqrt_deg[:, :], bank[2][:, 0:NB], ACT.Ln, bias=1.0), u)
        S.do(lambda e: e.activation(inv_sqrt_deg[:, :], inv_sqrt_deg[:, :], ACT.Exp, scale=-0.5), q)

        bias_fold, v_folds = {}, []
        for k, (mat, row) in enumerate((("L1_gnn_We2", "L1_gnn_be2"), ("L1_gnn_W3", "L1_gnn_b3"))):
            bias_fold[row] = sb("fold_" + row, [P, D])
            u = T.do(lambda e, k=k, mat=mat: e.matmul(bank[3][:, k * P:(k + 1) * P], ones[:, :], mats[mat][:, :],
                                                      start=True, stop=True), *v_folds[-1:])
            v_folds.append(None)
            v_fold = V.do(lambda e, k=k, row=row: e.scalar_tensor_tensor(
                bias_fold[row][:, :], bank[3][:, k * P:(k + 1) * P], -LOG2, rows[row][:, :], ALU.mult, ALU.add), u)
            v_folds[-1] = v_fold
        gcn_w = sb("gcn_w", [P, D])
        u = T.do(lambda e: e.transpose(bank[3][:, 2 * P:3 * P], mats["L2_gnn_W"][:, :], ident[:, :]), v_folds[-1])
        S.do(lambda e: e.copy(gcn_w[:, :], bank[3][:, 2 * P:3 * P]), u)

        rows_out = [sb_ring(f"rows_out{k}", [P, GRP, D]) for k in range(2)]
        norm, dense = Norm(), Dense(bank[4:6], bank[6:8], xt)
        rows_sem = [sem(f"rows{k}") for k in range(2)]
        zeroed, row_ready = {}, {}

        edge_row = sb_ring("edge_row", [P, ER, D + 1])
        edge_sem = [sem(f"edge_slot{k}") for k in range(ER)]
        edge_at = {}
        oh, tr, ev, hid, sp, fil, msg, po, sm = ({} for _ in range(9))

        def cf_edges(t):
            for s in range(GRP):
                i = t * GRP + s
                slot = i % ER
                edge_at[i] = G.dma(lambda e, i=i, slot=slot: e.indirect_dma_start(
                    out=edge_row[:, slot, :], out_offset=None, in_=edge_table,
                    in_offset=bass.IndirectOffsetOnAxis(ap=pick[1][:, i:i + 1], axis=0)),
                    (edge_sem[slot], 16 * (i // ER + 1)), *copied[-2:], *get(tr, t - ER // GRP),
                    *([landed_at[i - ER]] if i >= ER else []))

        ahead_ticks = ER // GRP
        for t in range(ahead_ticks):
            cf_edges(t)

        def n1_res(n):
            b0, b1 = span(n)
            q = V.do(lambda e: e.tensor_tensor(xb[n % 2][:, 0:b1 - b0, :], x_sb[:, b0:b1, :],
                                               rows["L0_gnn_bias"][:, :].unsqueeze(1).to_broadcast([P, b1 - b0, D]),
                                               ALU.add))
            for k, b in enumerate(sets[n]):
                p = V.do(lambda e, k=k, b=b: e.scalar_tensor_tensor(
                    res[n % 4][:, k, :], acc[:, b, 0:D], inv_den[:, b:b + 1], xb[n % 2][:, k, :], ALU.mult, ALU.add),
                    q, v_den, *get(norm.x, n - 4))
            zeroed[n] = G.do(lambda e: e.memset(acc[:, b0:b1, 0:D], 0.0), p)
            norm.stats(n, p)

        def n1_rows(n):
            b0, b1 = span(n)
            wid = (b1 - b0) * P
            row_ready[n] = S.do(lambda e: e.copy(rows_out[n % 2][:, 0:b1 - b0, :],
                                                 dense.bo[n % 2][:, 0:wid].rearrange("p (b d) -> p b d", d=D)),
                                dense.mm[n], *([(rows_sem[n % 2], 16 * (n // 2))] if n > 1 else []))
            dense.used[n] = row_ready[n]
            Y.dma(lambda e: e.dma_start(node_table[0][b0 * P:b1 * P, :].rearrange("(b p) d -> p b d", p=P),
                                        rows_out[n % 2][:, 0:b1 - b0, :]),
                  (rows_sem[n % 2], 16 * (n // 2 + 1)), row_ready[n])

        pipeline(NS, lagged([n1_res, norm.root, norm.invert, norm.scale,
                      lambda n: dense.turn(n, lambda b: x_sb[:, b, :], norm.x[n]), dense.keep,
                      lambda n: dense.times(n, mats["L1_gnn_Wn"]), n1_rows]))
        table_marks = [(rows_sem[(NS - 1 - k) % 2], 16 * ((NS - 1 - k) // 2 + 1)) for k in range(2)]
        barrier()

        edge_t = [sb_ring(f"edge_t{k}", [P, GRP * P]) for k in range(2)]
        magn = [sb_ring(f"magn{k}", [P, GRP * P]) for k in range(2)]
        plus = [sb_ring(f"plus{k}", [P, GRP * P]) for k in range(2)]
        message = [sb_ring(f"message{k}", [P, GRP, D]) for k in range(2)]
        be1 = cols["L1_gnn_be1"]

        def cf_nodes(t):
            for s in range(GRP):
                i = t * GRP + s
                slot = i % RING
                landed_at[i] = gather(slot, gathered[:, slot, 0:D], node_table[0],
                                      edge_row[:, i % ER, D:D + 1].bitcast(I32), edge_at[i], *table_marks,
                                      *get(msg, t - RING // GRP))

        def cf_turn(t):
            for s in range(GRP):
                i = t * GRP + s
                tr[t] = T.do(lambda e, s=s, i=i: e.transpose(bank[t % 2][:, s * P:(s + 1) * P],
                                                             edge_row[:, i % ER, 0:D], ident[:, :]),
                             edge_at[i], *get(ev, t - 2), quiet=(s < GRP - 1))

        def cf_keep(t):
            ev[t] = S.do(lambda e: e.copy(edge_t[t % 2][:, :], bank[t % 2][:, :]), tr[t], *get(hid, t - 2))

        def cf_hidden(t):
            hid[t] = T.do(lambda e: e.matmul(bank[2 + t % 2][:, :], mats["L1_gnn_We1"][:, :], edge_t[t % 2][:, :],
                                             start=True, stop=True), ev[t], *get(sp, t - 2))

        def cf_softplus(t):
            m, bk = magn[t % 2], bank[2 + t % 2]
            q0 = S.do(lambda e: e.activation(m[:, :], bk[:, :], ACT.Abs, bias=be1[:, 0:1]), hid[t], *get(sp, t - 2))
            q = S.do(lambda e: e.activation(m[:, :], m[:, :], ACT.Exp, scale=-1.0), q0)
            q = S.do(lambda e: e.activation(m[:, :], m[:, :], ACT.Ln, bias=1.0), q)
            r = V.do(lambda e: e.tensor_scalar(plus[t % 2][:, :], bk[:, :], be1[:, 0:1], 0.0, ALU.add, ALU.max),
                     q0, *get(fil, t - 2))
            sp[t] = V.do(lambda e: e.tensor_tensor(plus[t % 2][:, :], plus[t % 2][:, :], m[:, :], ALU.add), q, r)

        def cf_filter(t):
            bk = bank[4 + t % 2]
            T.do(lambda e: e.matmul(bk[:, :], ones[0:1, :], bias_fold["L1_gnn_be2"][0:1, :].unsqueeze(1)
                                    .to_broadcast([1, GRP, D]), start=True, stop=False), *get(msg, t - 2), quiet=True)
            for s in range(GRP):
                fil[t] = T.do(lambda e, s=s: e.matmul(bk[:, s * P:(s + 1) * P], plus[t % 2][:, s * P:(s + 1) * P],
                                                      mats["L1_gnn_We2"][:, :], start=False, stop=(s == GRP - 1)),
                              sp[t], quiet=(s < GRP - 1))

        def cf_message(t):
            i, s0 = t * GRP, slots(t)[0]
            msg[t] = V.do(lambda e: e.tensor_tensor(message[t % 2][:, :, :], bank[4 + t % 2][:, :]
                                                    .rearrange("p (s d) -> p s d", s=GRP),
                                                    gathered[:, s0:s0 + GRP, 0:D], ALU.mult),
                          fil[t], *landed(t), *get(po, t - 2))
            yield
            oh[t] = V.do(lambda e: e.tensor_tensor(
                hot[t % 2][:, :, :], iota_free[:, :].unsqueeze(1).to_broadcast([P, GRP, P]),
                local[1][:, i:i + GRP].unsqueeze(2).to_broadcast([P, GRP, P]), ALU.is_equal), *get(po, t - 2))
            yield

        def cf_product(t):
            for s in range(GRP):
                po[t] = T.do(lambda e, s=s: e.matmul(bank[6 + t % 2][:, s * P:(s + 1) * P], hot[t % 2][:, s, :],
                                                     message[t % 2][:, s, :], start=True, stop=True),
                             msg[t], oh[t], *get(sm, t - 2), quiet=(s < GRP - 1))

        def plain_sum(which, po, sm):
            def stage(t):
                block_registers(which, t)
                q = None
                for s in range(GRP):
                    i = t * GRP + s
                    o = bank[6 + t % 2][:, s * P:(s + 1) * P]

                    def add(e, i=i, o=o):
                        a = block_sum(e, i, D)
                        return e.tensor_tensor(a, a, o, ALU.add)
                    q = V.do(add, po[t], *([q] if q else get(sm, t - 1)))
                    yield
                sm[t] = q
            return stage

        pipeline(TICKS, [(9, plain_sum(1, po, sm), True), (7, cf_message, True), (8, cf_product, False),
                         (6, cf_filter, False), (5, cf_softplus, False), (4, cf_hidden, False),
                         (3, cf_keep, False), (2, cf_turn, False), (1, cf_nodes, False), (0, lambda t: t >= ahead_ticks and cf_edges(t), False)])
        barrier()

        first, norm = Dense(bank[0:2], bank[2:4], xt), Norm(logs=True)
        sp_n, rel_n, res_n = {}, {}, {}
        third_buf = [sb_ring(f"third_buf{k}", [P, GRP * P]) for k in range(2)]
        third = Dense([bank[5]] * 2, bank[6:8], third_buf)
        m_t1 = (sem("table1_out"), 16 * NS)

        def n2_softplus(n):
            wid = len(sets[n]) * P
            m, r, bk = magn[n % 2], plus[n % 2], bank[2 + n % 2]
            col = cols["L1_gnn_b2"]
            q0 = S.do(lambda e: e.activation(m[:, 0:wid], bk[:, 0:wid], ACT.Abs, bias=col[:, 0:1]), first.mm[n],
                      *get(sp_n, n - 2))
            q = S.do(lambda e: e.activation(m[:, 0:wid], m[:, 0:wid], ACT.Exp, scale=-1.0), q0)
            q = S.do(lambda e: e.activation(m[:, 0:wid], m[:, 0:wid], ACT.Ln, bias=1.0), q)
            r0 = V.do(lambda e: e.tensor_scalar(r[:, 0:wid], bk[:, 0:wid], col[:, 0:1], 0.0, ALU.add, ALU.max),
                      q0, *get(rel_n, n - 2))
            sp_n[n] = V.do(lambda e: e.tensor_tensor(r[:, 0:wid], r[:, 0:wid], m[:, 0:wid], ALU.add), q, r0)
            first.used[n] = sp_n[n]

        def second_times(n, buf, ready, mat, bias_row, done, used):
            cnt = len(sets[n])
            T.do(lambda e: e.matmul(bank[4][:, 0:cnt * P], ones[0:1, :],
                                    bias_row[0:1, :].unsqueeze(1).to_broadcast([1, cnt, D]), start=True, stop=False),
                 *get(used, n - 1), quiet=True)
            for k in range(cnt):
                done[n] = T.do(lambda e, k=k: e.matmul(bank[4][:, k * P:(k + 1) * P], buf[n % 2][:, k * P:(k + 1) * P],
                                                       mat[:, :], start=False, stop=(k == cnt - 1)),
                               ready, quiet=(k < cnt - 1))

        def n2_res(n):
            b0, b1 = span(n)
            wid = (b1 - b0) * P
            res_n[n] = V.do(lambda e: e.scalar_tensor_tensor(
                res[n % 4][:, 0:b1 - b0, :], x_sb[:, b0:b1, :], 2.0,
                bank[4][:, 0:wid].rearrange("p (b d) -> p b d", d=D), ALU.mult, ALU.add), rel_n[n])
            norm.stats(n, res_n[n])

        def n2_rows(n):
            b0, b1 = span(n)
            third.used[n] = V.do(lambda e: e.tensor_tensor(
                acc[:, b0:b1, 0:D], bank[6 + n % 2][:, 0:(b1 - b0) * P].rearrange("p (b d) -> p b d", d=D),
                inv_sqrt_deg[:, b0:b1].unsqueeze(2).to_broadcast([P, b1 - b0, D]), ALU.mult),
                third.mm[n], first.tr[n])
            Y.dma(lambda e: e.dma_start(node_table[1][b0 * P:b1 * P, :].rearrange("(b p) d -> p b d", p=P),
                                        acc[:, b0:b1, 0:D]), m_t1, third.used[n])

        pipeline(NS, lagged([lambda n: first.turn(n, lambda b: acc[:, b, 0:D]), first.keep,
                      lambda n: first.columns(n, mats["L1_gnn_W2"]), n2_softplus,
                      lambda n: second_times(n, plus, sp_n[n], mats["L1_gnn_W3"], bias_fold["L1_gnn_b3"], rel_n, res_n),
                      n2_res, norm.root, norm.scale,
                      lambda n: third.turn(n, lambda b: x_sb[:, b, :], norm.x[n], *get(third.ev, n - 1)), third.keep,
                      lambda n: third.times(n, gcn_w), n2_rows]))
        barrier()

        def plain_layer(table, ready):
            oh, po, sm = {}, {}, {}

            def fetch(t):
                for s in range(GRP):
                    i = t * GRP + s
                    landed_at[i] = gather(i % RING, gathered[:, i % RING, 0:D], table, pick[0][:, i:i + 1], ready,
                                          *get(po, t - RING // GRP))

            def one_hot(t):
                i = t * GRP
                oh[t] = V.do(lambda e: e.tensor_tensor(
                    hot[t % 2][:, :, :], iota_free[:, :].unsqueeze(1).to_broadcast([P, GRP, P]),
                    local[0][:, i:i + GRP].unsqueeze(2).to_broadcast([P, GRP, P]), ALU.is_equal), *get(po, t - 2))

            def product(t):
                for s, slot in enumerate(slots(t)):
                    po[t] = T.do(lambda e, s=s, slot=slot: e.matmul(
                        bank[6 + t % 2][:, s * P:(s + 1) * P], hot[t % 2][:, s, :], gathered[:, slot, 0:D],
                        start=True, stop=True), oh[t], landed_at[t * GRP + s], *get(sm, t - 2), quiet=(s < GRP - 1))

            pipeline(TICKS, [(3, plain_sum(0, po, sm), True), (2, product, False), (1, one_hot, False),
                             (0, fetch, False)])

        plain_layer(node_table[1], m_t1)
        barrier()

        norm = Norm()
        m_t2 = (sem("table2_out"), 16 * NS)

        def n3_res(n):
            b0, b1 = span(n)
            q = V.do(lambda e: e.tensor_tensor(xb[n % 2][:, 0:b1 - b0, :], x_sb[:, b0:b1, :],
                                               rows["L2_gnn_b"][:, :].unsqueeze(1).to_broadcast([P, b1 - b0, D]),
                                               ALU.add))
            for k, b in enumerate(sets[n]):
                p = V.do(lambda e, k=k, b=b: e.scalar_tensor_tensor(
                    res[n % 4][:, k, :], acc[:, b, 0:D], inv_sqrt_deg[:, b:b + 1], xb[n % 2][:, k, :],
                    ALU.mult, ALU.add), q, *get(norm.x, n - 4))
            norm.stats(n, p)

        def n3_rows(n):
            b0, b1 = span(n)
            S.do(lambda e: e.copy(acc[:, b0:b1, 0:D], x_sb[:, b0:b1, :]), norm.x[n])
            Y.dma(lambda e: e.dma_start(node_table[2][b0 * P:b1 * P, :].rearrange("(b p) d -> p b d", p=P),
                                        x_sb[:, b0:b1, :]), m_t2, norm.x[n])

        pipeline(NS, lagged([n3_res, norm.root, norm.invert, norm.scale, n3_rows]))
        barrier()
        plain_layer(node_table[2], m_t2)
        barrier()

        first, norm = Dense(bank[0:2], bank[2:4], xt), Norm()
        act_n, rel_n, res_n = {}, {}, {}
        m_out = (sem("out_written"), 16 * NS)

        def n4_relu(n):
            wid = len(sets[n]) * P
            act_n[n] = S.do(lambda e: e.activation(plus[n % 2][:, 0:wid], bank[2 + n % 2][:, 0:wid], ACT.Relu,
                                                   bias=cols["L3_gnn_b1"][:, 0:1]), first.mm[n], *get(rel_n, n - 2))
            first.used[n] = act_n[n]

        def n4_res(n):
            b0, b1 = span(n)
            wid = (b1 - b0) * P
            res_n[n] = V.do(lambda e: e.tensor_tensor(
                res[n % 4][:, 0:b1 - b0, :], x_sb[:, b0:b1, :],
                bank[4][:, 0:wid].rearrange("p (b d) -> p b d", d=D), ALU.add), rel_n[n], *get(norm.x, n - 4))
            norm.stats(n, res_n[n])

        def n4_store(n):
            b0, b1 = span(n)
            if b1 < NB:
                Y.dma(lambda e: e.dma_start(out[b0 * P:b1 * P, :].rearrange("(b p) d -> p b d", p=P),
                                            x_sb[:, b0:b1, :]), m_out, norm.x[n])
            else:
                assert b1 - b0 == 1
                Y.dma(lambda e: e.dma_start(out[b0 * P:N, :], x_sb[0:LAST, b0, :]), m_out, norm.x[n])

        pipeline(NS, lagged([lambda n: first.turn(n, lambda b: acc[:, b, 0:D]), first.keep,
                      lambda n: first.columns(n, mats["L3_gnn_W1"]), n4_relu,
                      lambda n: second_times(n, plus, act_n[n], mats["L3_gnn_W2"], rows["L3_gnn_b2"], rel_n, res_n),
                      n4_res, norm.root, norm.invert, norm.scale, n4_store]))
        Y.items.append(((m_x, m_w, m_out, m_t1, m_t2, *table_marks, *copied[-2:]), None, None))
        finish(nc, ctx, V, S, T, G, Y)


def finish(nc, ctx, V, S, T, G, Y):
    block = ctx.enter_context(nc.Block())
    block.vector(V.play)
    block.scalar(S.play)
    block.tensor(T.play)
    block.gpsimd(G.play)
    block.sync(Y.play)


INPUTS = ["x", "src", "dst", "edge_attr_128", "L0_gnn_W", "L0_gnn_att_src", "L0_gnn_att_dst", "L0_gnn_bias",
          "L1_gnn_Wn", "L1_gnn_We1", "L1_gnn_be1", "L1_gnn_We2", "L1_gnn_be2", "L1_gnn_W2", "L1_gnn_b2",
          "L1_gnn_W3", "L1_gnn_b3", "L2_gnn_W", "L2_gnn_b", "L3_gnn_W1", "L3_gnn_b1", "L3_gnn_W2", "L3_gnn_b2"]


def kernel(**inputs):
    import numpy as np
    import concourse.bacc as bacc
    from concourse.bass_utils import run_bass_kernel_spmd as run

    nc = bacc.Bacc("TRN2", target_bir_lowering=False, num_devices=1)
    arrays, args = {}, {}
    for name in INPUTS:
        arrays[name] = np.ascontiguousarray(inputs[name])
        args[name] = nc.dram_tensor(name, arrays[name].shape, mybir.dt.from_np(arrays[name].dtype),
                                    kind="ExternalInput").ap()
    out = nc.dram_tensor("out", (N, D), F32, kind="ExternalOutput").ap()
    build_program(nc, args, out)
    return run(nc, [arrays], core_ids=[0]).results[0]["out"]
```
